# Optimizing a Trainium2 kernel written in Bass

```python
import numpy as np
import jax
import jax.numpy as jnp

def _softmax(x, axis=-1):
    return jax.nn.softmax(x, axis=axis)

def _gelu(x):
    return jax.nn.gelu(x, approximate=True)

def _silu(x):
    return jax.nn.silu(x)

def _sigmoid(x):
    return jax.nn.sigmoid(x)

def _layernorm(x, axis=-1, eps=1e-05):
    m = jnp.mean(x, axis=axis, keepdims=True)
    v = jnp.var(x, axis=axis, keepdims=True)
    return (x - m) / jnp.sqrt(v + eps)

def _scatter_add(tgt, idx, src, axis=0):
    return tgt.at[idx].add(src)

def _segment_sum(src, seg, n):
    return jax.ops.segment_sum(src, seg, n)
kernel_name = 'mk_adj_resnorm_d1_adj_r2_1f7e69'

def setup_inputs(seed: int=0):
    np.random.seed(seed)
    _w = jnp.asarray

    def _rec_inputs():
        import jax
        import jax.numpy as jnp
        _gk = jax.random.key(seed)
        x = -0.0001071 + 1.001 * jax.random.normal(jax.random.fold_in(_gk, 1), (8, 1500, 64), jnp.float32)
        _w = (1.0 + jnp.arange(1500, dtype=jnp.float32)) ** (-0.5)
        _w = _w / _w.mean()
        _pij = jnp.clip(0.0106667 * _w[:, None] * _w[None, :], 0.0, 1.0)
        _a = jax.random.uniform(jax.random.fold_in(_gk, 2), (8, 1500, 1500)) < _pij
        _af = _a.astype(jnp.float32)
        adj = _af
        return (x, adj)
    x, adj = _rec_inputs()

    def _L0_gnn_setup():
        import jax, jax.numpy as jnp
        import numpy as np
        B, N, F = (2, 1500, 64)
        H, OUT, ATT = (4, 16, 16)
        DENSITY = 0.01
        key = jax.random.key(seed)
        ks = jax.random.split(key, 6)
        h = jax.random.normal(ks[0], (B, N, F), dtype=jnp.float32)
        a = (jax.random.uniform(ks[1], (B, N, N)) < DENSITY).astype(jnp.float32)
        glorot = lambda k, shape: jax.random.uniform(k, shape, jnp.float32, -1.0, 1.0) * jnp.sqrt(6.0 / (shape[-2] + shape[-1]))
        kernel = glorot(ks[2], (H, F, OUT))
        attention_kernel = glorot(ks[3], (H, F, ATT))
        attention_kernel_2 = glorot(ks[4], (H, F, ATT))
        bias = jax.random.normal(ks[5], (1, 1, H, OUT), dtype=jnp.float32) * 0.01
        return {'h': h, 'a': a, 'kernel': kernel, 'attention_kernel': attention_kernel, 'attention_kernel_2': attention_kernel_2, 'bias': bias}
    _L0_gnn_all = _L0_gnn_setup()
    _L0_gnn_in = {k: v for k, v in _L0_gnn_all.items() if k in ('kernel', 'attention_kernel', 'attention_kernel_2', 'bias')}
    del _L0_gnn_all
    return {'x': x, 'adj': adj, 'L0_gnn_kernel': _L0_gnn_in['kernel'], 'L0_gnn_attention_kernel': _L0_gnn_in['attention_kernel'], 'L0_gnn_attention_kernel_2': _L0_gnn_in['attention_kernel_2'], 'L0_gnn_bias': _L0_gnn_in['bias']}

def reference(x, adj, L0_gnn_kernel, L0_gnn_attention_kernel, L0_gnn_attention_kernel_2, L0_gnn_bias):
    import jax
    import jax.numpy as jnp

    def _L0_gnn_ref(h, a, kernel, attention_kernel, attention_kernel_2, bias):
        import jax, jax.numpy as jnp
        import numpy as np
        B, N, F = (2, 1500, 64)
        H, OUT, ATT = (4, 16, 16)
        DENSITY = 0.01
        feats = jnp.einsum('bnf,hfo->bhno', h, kernel)
        f_self = jnp.einsum('bnf,hfd->hbnd', h, attention_kernel)
        f_other = jnp.einsum('bnf,hfd->hbdn', h, attention_kernel_2)
        a_h = a[None]
        scores = jnp.einsum('hbnd,hbdm->hbnm', f_self, f_other)
        masked = a_h * scores
        masked = jnp.where(masked >= 0, masked, 0.2 * masked)
        masked = masked / jnp.sqrt(jnp.float32(ATT))
        masked = masked + jnp.where(a_h == 0, jnp.float32(-1000000000.0), jnp.float32(0.0))
        attn = jax.nn.softmax(masked, axis=-1)
        attn = attn * jnp.where(a_h == 0, jnp.float32(0.0), jnp.float32(1.0))
        attn = jnp.transpose(attn, (1, 0, 2, 3))
        node_features = jnp.einsum('bhnm,bhmo->bhno', attn, feats)
        node_features = node_features + jnp.transpose(bias, (0, 2, 1, 3))
        node_features = jax.nn.relu(node_features)
        node_features = jnp.transpose(node_features, (0, 2, 1, 3))
        return node_features.reshape(-1, N, H * OUT)
    x = _layernorm(x + _L0_gnn_ref(x, adj, L0_gnn_kernel, L0_gnn_attention_kernel, L0_gnn_attention_kernel_2, L0_gnn_bias), axis=-1)
    return x

_drawn_inputs = setup_inputs


def setup_inputs(seed=0):
    import zlib

    import numpy as np

    out = dict(_drawn_inputs(seed))
    spreads = {}
    factors = {'L0_gnn_bias': 7.56}
    for name, (base, spread) in spreads.items():
        noise = np.random.default_rng([zlib.crc32(name.encode()), seed]).standard_normal(out[name].shape)
        drawn = base * np.exp(spread * noise) if base else spread * noise
        out[name] = jnp.asarray(drawn.astype(out[name].dtype))
    for name, factor in factors.items():
        out[name] = (out[name] * factor).astype(out[name].dtype)
    return out
```

```python
from contextlib import ExitStack

import concourse.bass as bass
from concourse import mybir

F32 = mybir.dt.float32
BF16 = mybir.dt.bfloat16
I32 = mybir.dt.int32
ALU = mybir.AluOpType
ACT = mybir.ActivationFunctionType
AX_X = mybir.AxisListType.X

P = 128
B, N, F, H, D = 8, 1500, 64, 4, 16
T = 125
NT = N // T
SJ = 4
W = SJ * T
NS = NT // SJ
NPAD = 1536
PAIRS = 2 * NT
QB = NS * PAIRS
HF = H * D
OW = 32
BIG = 2.0 ** 100
GAIN = 4.0
SCALE = 0.05
EPS = 1e-5
SELF_PART = (0, 0, 1, 1, 0, 2)
OTHER_PART = (0, 1, 0, 1, 2, 0)
KR = D * len(SELF_PART)
SAFE = 60.0

ROOT_STEPS = 3
NEWTON = NS + 2 + 3 * ROOT_STEPS
SPLITS = 6
MAXIMA = NT * H
PARTS = 7
CONSTS = 13
STACK_DMAS = 2 * H * len(SELF_PART)
XT_ROUNDS = 2
PROJ_ROUNDS = XT_ROUNDS + NS
VALS_ROUNDS = PROJ_ROUNDS + 2
PREP_ROUNDS = VALS_ROUNDS + 3
PREP_AT = [*range(4, 4 + 2 * VALS_ROUNDS, 2), 40, 43, 46]
OUT_AT = [PAIRS * (s + 1) + 4 for s in range(NS - 1)]
FINISH_AFTER = (2, 6, 7, 8, 9, 10, 11, 12, 18)
ROUNDS = PREP_ROUNDS + NS


def gat_layer(nc, x, adj, w_feat, w_self, w_other, bias, out):
    with ExitStack() as ctx:
        def sb(name, shape, dt):
            return ctx.enter_context(nc.sbuf_tensor(name, shape, dt))

        def sem(name):
            return ctx.enter_context(nc.semaphore(name))

        w_proj = sb("w_proj", [F, 2 * HF], F32)
        w_val = sb("w_val", [F, HF], F32)
        bias_rep = sb("bias_rep", [P, HF], F32)
        ident = sb("ident", [P, P], F32)
        head_sum = sb("head_sum", [P, 2 * H], F32)
        x_sb = [sb(f"x_sb{p}", [P, NT, F], F32) for p in range(2)]
        xT = sb("xT", [F, N], F32)
        proj = sb("proj", [P, N], F32)
        rest = sb("rest", [P, N], F32)
        parts = [sb(f"part{k}", [P, N], BF16) for k in range(3)]
        self_st = [sb(f"self_st{p}", [KR, H, N], BF16) for p in range(2)]
        other_st = [sb(f"other_st{p}", [KR, H, NPAD], BF16) for p in range(2)]
        vals = [sb(f"vals{p}", [P, NT, H, OW], F32) for p in range(2)]
        stage = sb("stage", [P, SJ, N], F32)
        am1 = [sb(f"am1_{k}", [P, SJ, NPAD], BF16) for k in range(2)]
        shift = sb("shift", [P, H, NT, T], BF16)
        probs = sb("probs", [P, 3, H, W], F32)
        relu_dve = sb("relu_dve", [P, 2, W], F32)
        o_sb = sb("o_sb", [P, W], F32)
        den = sb("den", [P, SJ * H], F32)
        rden = sb("rden", [P, SJ * H], F32)
        ob = sb("ob", [P, SJ, HF], F32)
        yb = sb("yb", [P, SJ, HF], F32)
        sq = sb("sq", [P, SJ, HF], F32)
        mean = sb("mean", [P, SJ], F32)
        cent = [sb(f"cent{p}", [P, NT, HF], F32) for p in range(2)]
        var = sb("var", [P, NT], F32)
        rstd = sb("rstd", [P, NT], F32)
        nwt = sb("nwt", [P, NT], F32)

        norm = sb("norm", [P, P], F32)
        norm_t = sb("norm_t", [P, P], F32)
        flag_f = sb("flag_f", [P, 4], F32)
        safe = [sb(f"safe{p}", [1, 1], I32) for p in range(2)]
        row_max = sb("row_max", [P, P], F32)
        row_tmp = sb("row_tmp", [P, P], F32)
        max_part = [sb(f"max_part{k}", [MAXIMA, T], BF16) for k in range(3)]
        zero_row = sb("zero_row", [P, T], BF16)

        z = ctx.enter_context(nc.psum_tensor("z", [P, 6, 512], F32))
        numer = ctx.enter_context(nc.psum_tensor("numer", [P, 512], F32))
        misc = ctx.enter_context(nc.psum_tensor("misc", [P, 512], F32))

        weights_in = sem("weights_in")
        x_in = sem("x_in")
        stage_in = [sem(f"stage_in{j}") for j in range(SJ)]
        stage_free = sem("stage_free")
        consts = sem("consts")
        misc_full = sem("misc_full")
        misc_free = sem("misc_free")
        splits = sem("splits")
        stacks_in = sem("stacks_in")
        scored = sem("scored")
        half = sem("half")
        leaky_act = sem("leaky_act")
        leaky_dve = sem("leaky_dve")
        masked = sem("masked")
        expd = sem("expd")
        pv_done = sem("pv_done")
        numer_free = sem("numer_free")
        resid = sem("resid")
        squared = sem("squared")
        epi = sem("epi")
        mean_ready = sem("mean_ready")
        centered = sem("centered")
        newton = sem("newton")
        rstd_ready = sem("rstd_ready")
        normed = sem("normed")
        shift_ready = sem("shift_ready")
        pads = sem("pads")
        am1_init = sem("am1_init")
        flag = sem("flag")
        safe_ready = sem("safe_ready")
        big_adj_in = sem("big_adj_in")
        big_scored = sem("big_scored")
        big_read = sem("big_read")
        big_max = sem("big_max")
        big_turned = sem("big_turned")
        big_parts = sem("big_parts")
        shift_in = sem("shift_in")
        shift_zeroed = sem("shift_zeroed")
        gate = sem("gate")
        stored = [sem(f"stored{p}") for p in range(2)]

        block = ctx.enter_context(nc.Block())

        def at(i, par, per, n):
            return i * (2 * per) + (par * per + n)

        NEXT = lambda i, par: 2 * i + 1 if par == 0 else (2 * i + 2) % B

        @block.sync
        def _(sp):
            def load_x(b, buf):
                sp.dma_start(x_sb[buf][0:T, :, :],
                             x[b, :, :].rearrange("(j p) f -> p j f", p=T)).then_inc(x_in, 16)

            def load_adj(b, tile, j):
                sp.dma_start(stage[0:T, j, :], adj[b, tile * T:(tile + 1) * T, :]).then_inc(stage_in[j], 16)

            def stack(buf):
                for g in range(len(SELF_PART)):
                    for h in range(H):
                        rows = slice(g * D, (g + 1) * D)
                        sp.dma_start(self_st[buf][rows, h, :],
                                     parts[SELF_PART[g]][h * D:(h + 1) * D, :]).then_inc(stacks_in, 16)
                        sp.dma_start(other_st[buf][rows, h, 0:N],
                                     parts[OTHER_PART[g]][HF + h * D:HF + (h + 1) * D, :]).then_inc(stacks_in, 16)

            sp.sem_inc(shift_zeroed, 16)
            sp.sem_inc(stored[0], 16)
            sp.sem_inc(stored[1], 16)
            load_x(0, 0)
            sp.dma_start(w_proj[:, 0:HF].rearrange("f (h d) -> f h d", h=H),
                         w_self.rearrange("h f d -> f h d")).then_inc(weights_in, 16)
            sp.dma_start(w_proj[:, HF:2 * HF].rearrange("f (h d) -> f h d", h=H),
                         w_other.rearrange("h f d -> f h d")).then_inc(weights_in, 16)
            sp.dma_start(w_val[:, :].rearrange("f (h d) -> f h d", h=H),
                         w_feat.rearrange("h f d -> f h d")).then_inc(weights_in, 16)
            sp.dma_start(bias_rep[:, :],
                         bias.rearrange("a b h d -> (a b) (h d)").broadcast_to([P, HF])).then_inc(weights_in, 16)
            for j in range(SJ):
                load_adj(0, j, j)
            sp.wait_ge(splits, SPLITS - 1)
            sp.wait_ge(consts, CONSTS)
            stack(0)
            def shift_rows(k):
                return shift[T + k:T + k + 1, :, :, :].rearrange("p h j n -> p (h j) n")

            def large_scores(i, par):
                with sp.Fori(0, NT) as t:
                    sp.wait_ge(big_read, at(i, par, MAXIMA, 1) + t * H)
                    sp.dma_start(rest[0:T, :], adj[2 * i + par, bass.ts(t, T), :]).then_inc(big_adj_in, 16)
                sp.wait_ge(big_parts, at(i, par, PARTS, PARTS))
                for k in range(3):
                    sp.dma_start(shift_rows(k), max_part[k][:, :]).then_inc(shift_in, 16)

            with sp.Fori(0, B // 2) as i:
                for par in range(2):
                    sp.wait_ge(safe_ready, at(i, par, 1, 1))
                    sp.sem_inc(gate, 1)
                    small = sp.value_load(safe[par][0:1, 0:1], min_val=0, max_val=1)
                    with sp.If(small == 0):
                        large_scores(i, par)
                    with sp.Else():
                        sp.sem_inc(big_adj_in, 16 * NT)
                        sp.sem_inc(shift_in, 16 * 3)
                    sp.wait_ge(resid, at(i, par, NS, 1))
                    load_x(NEXT(i, par), 1 - par)
                    for st in range(NS):
                        last = st == NS - 1
                        for j in range(SJ):
                            sp.wait_ge(stage_free, at(i, par, NT, st * SJ + j + SJ + 1))
                            load_adj(NEXT(i, par) if last else 2 * i + par, j if last else (st + 1) * SJ + j, j)
                        if st == 1:
                            sp.wait_ge(splits, at(i, par, SPLITS, 2 * SPLITS - 1))
                            stack(1 - par)
                    with sp.If(small == 0):
                        sp.wait_ge(masked, at(i, par, QB, QB + 1))
                        sp.dma_start(shift[T:P, :, :, :].rearrange("p h j n -> p (h j) n"),
                                     zero_row[0:3, :].unsqueeze(1).broadcast_to([3, MAXIMA, T])
                                     ).then_inc(shift_zeroed, 16)
                    with sp.Else():
                        sp.sem_inc(shift_zeroed, 16)
                    sp.wait_ge(normed, at(i, par, 1, 2))
                    sp.dma_start(out[2 * i + par, :, :].rearrange("(j p) f -> p j f", p=T),
                                 cent[par][0:T, :, :]).then_inc(stored[par], 16)
            for p in range(2):
                sp.wait_ge(stored[p], 16 * (B // 2) + 16)
            sp.wait_ge(shift_zeroed, 16 * (B + 1))
            sp.wait_ge(stacks_in, 16 * STACK_DMAS * (B + 1))

        @block.gpsimd
        def _(pool):
            pool.sem_inc(stage_free, SJ)
            pool.sem_inc(normed, 1)
            pool.memset(ident[:, :], 0.0).then_inc(consts, 1)
            pool.memset(head_sum[:, :], 1.0).then_inc(consts, 1)
            pool.memset(shift[:, :, :, :], 0.0).then_inc(consts, 1)
            for p in range(2):
                pool.memset(vals[p][:, :, :, :], 0.0).then_inc(consts, 1)
                pool.memset(other_st[p][:, :, N:NPAD], 0.0).then_inc(consts, 1)
            pool.memset(zero_row[:, :], 0.0).then_inc(consts, 1)
            pool.wait_ge(consts, 8)
            pool.affine_select(out=ident[:, :], in_=ident[:, :], compare_op=ALU.not_equal, fill=1.0, base=0,
                               pattern=[[-1, P]], channel_multiplier=1).then_inc(consts, 1)
            pool.affine_select(out=head_sum[:, :], in_=head_sum[:, :], compare_op=ALU.is_ge, fill=0.0, base=0,
                               pattern=[[-D, 2 * H]], channel_multiplier=1).then_inc(consts, 1)
            for p in range(2):
                pool.memset(vals[p][:, :, :, D:D + 1], 1.0).then_inc(consts, 1)
            pool.wait_ge(consts, 12)
            pool.affine_select(out=head_sum[:, :], in_=head_sum[:, :], compare_op=ALU.is_ge, fill=0.0, base=D - 1,
                               pattern=[[D, 2 * H]], channel_multiplier=-1).then_inc(consts, 1)
            pool.affine_select(out=shift[:, :, :, :].rearrange("p h j n -> p (h j) n"),
                               in_=shift[:, :, :, :].rearrange("p h j n -> p (h j) n"),
                               compare_op=ALU.not_equal, fill=BIG, base=0, pattern=[[0, H * NT], [-1, T]],
                               channel_multiplier=1).then_inc(shift_ready, 1)
            for m in (norm, norm_t, row_max, row_tmp):
                pool.memset(m[:, :], 0.0).then_inc(pads, 1)
            pool.memset(am1[0][:, :, :], 1.0).then_inc(am1_init, 1)
            pool.memset(am1[1][:, :, :], 1.0).then_inc(am1_init, 1)
            pool.wait_ge(am1_init, 2)

            def convert(buf, j):
                pool.sem_inc(gate, 1)
                pool.tensor_scalar(am1[buf][0:T, j, 0:N], stage[0:T, j, :], -1.0, 1.0,
                                   ALU.add, ALU.mult).then_inc(stage_free, 1)

            def split(done):
                pool.sem_inc(gate, 1)
                pool.tensor_scalar(parts[0][:, :], proj[:, :], 1.0, 0.0, ALU.mult, ALU.add).then_inc(splits, 1)
                pool.wait_ge(splits, done + 1)
                pool.tensor_tensor(rest[:, :], proj[:, :], parts[0][:, :], ALU.subtract).then_inc(splits, 1)
                pool.wait_ge(splits, done + 2)
                pool.sem_inc(gate, 1)
                pool.tensor_scalar(parts[1][:, :], rest[:, :], 1.0, 0.0, ALU.mult, ALU.add).then_inc(splits, 1)
                pool.wait_ge(splits, done + 3)
                pool.tensor_tensor(rest[:, :], rest[:, :], parts[1][:, :], ALU.subtract).then_inc(splits, 1)
                pool.wait_ge(splits, done + 4)
                pool.sem_inc(gate, 1)
                pool.tensor_scalar(parts[2][:, :], rest[:, :], 1.0, 0.0, ALU.mult, ALU.add).then_inc(splits, 1)
                pool.wait_ge(splits, done + 5)
                pool.tensor_tensor(rest[:, :], proj[:, :], proj[:, :], ALU.mult).then_inc(splits, 1)

            def center(i, par, st):
                rows = cent[par][0:T, st * SJ:(st + 1) * SJ, :]
                pool.wait_ge(mean_ready, at(i, par, NS, st + 1))
                if st == 0:
                    pool.wait_ge(stored[par], 16 * i + 16)
                pool.tensor_tensor(rows, yb[0:T, :, :],
                                   mean[0:T, :].unsqueeze(2).broadcast_to([T, SJ, HF]),
                                   ALU.subtract).then_inc(centered, 1)
                pool.wait_ge(centered, at(i, par, NS, st + 1))
                pool.tensor_tensor(sq[0:T, :, :], rows, rows, ALU.mult).then_inc(squared, 1)

            pool.wait_ge(misc_free, 1 + PROJ_ROUNDS)
            split(0)
            for j in range(SJ):
                pool.wait_ge(stage_in[j], 16)
                convert(0, j)

            with pool.Fori(0, B // 2) as i:
                for par in range(2):
                    for st in range(NS):
                        pool.wait_ge(masked, at(i, par, QB, st * PAIRS + 1))
                        for j in range(SJ):
                            pool.wait_ge(stage_in[j], at(i, par, 16 * NS, 16 * (st + 2)))
                            convert((par * NS + st + 1) % 2, j)
                        if st == 0:
                            pool.wait_ge(misc_free, at(i, par, ROUNDS, PREP_ROUNDS + 1 + PROJ_ROUNDS))
                            pool.wait_ge(stacks_in, at(i, par, 16 * STACK_DMAS, 16 * STACK_DMAS))
                            split(at(i, par, SPLITS, SPLITS))
                        else:
                            center(i, par, st - 1)
                    center(i, par, NS - 1)
                    pool.wait_ge(rstd_ready, at(i, par, 1, 1))
                    pool.tensor_tensor(cent[par][0:T, :, :], cent[par][0:T, :, :],
                                       rstd[0:T, :].unsqueeze(2).broadcast_to([T, NT, HF]),
                                       ALU.mult).then_inc(normed, 1)

        @block.tensor
        def _(pe):
            pe.sem_inc(masked, 1)
            pe.wait_ge(consts, CONSTS)
            pe.wait_ge(weights_in, 64)

            def xT_round(buf, r, n):
                pe.wait_ge(misc_free, n)
                for k in range(3):
                    j = 6 * r + 2 * k
                    m = nc.tensor.transpose(misc[:, k * T:(k + 1) * T],
                                            x_sb[buf][0:T, j:j + 2, :].rearrange("p j f -> p (j f)"),
                                            ident[0:T, 0:T])
                m.then_inc(misc_full, 1)

            def proj_round(r, n):
                pe.wait_ge(misc_free, n)
                nc.tensor.matmul(misc[:, 0:W], w_proj[:, :], xT[:, r * W:(r + 1) * W],
                                 start=True, stop=True).then_inc(misc_full, 1)

            def vals_round(r, n):
                pe.wait_ge(misc_free, n)
                for c in range(8 * r, min(8 * r + 8, NT)):
                    m = nc.tensor.matmul(misc[0:T, (c - 8 * r) * HF:(c - 8 * r + 1) * HF], xT[:, c * T:(c + 1) * T],
                                         w_val[:, :], start=True, stop=True)
                m.then_inc(misc_full, 1)

            def norms_round(r, n, split_done):
                pe.wait_ge(misc_free, n)
                if r == 0:
                    pe.wait_ge(splits, split_done)
                    for c in range(NT):
                        m = nc.tensor.matmul(misc[0:T, c * 2 * H:(c + 1) * 2 * H], rest[:, c * T:(c + 1) * T],
                                             head_sum[:, :], start=True, stop=True)
                else:
                    m = nc.tensor.transpose(misc[:, 0:P], (norm if r == 1 else norm_t)[:, :], ident[:, :])
                m.then_inc(misc_full, 1)

            def prep_round(buf, r, n, split_done):
                if r < XT_ROUNDS:
                    xT_round(buf, r, n)
                elif r < PROJ_ROUNDS:
                    proj_round(r - XT_ROUNDS, n)
                elif r < VALS_ROUNDS:
                    vals_round(r - PROJ_ROUNDS, n)
                else:
                    norms_round(r - VALS_ROUNDS, n, split_done)

            def out_round(n):
                pe.wait_ge(misc_free, n)
                for j in range(SJ):
                    m = nc.tensor.transpose(misc[0:T, j * P:(j + 1) * P], o_sb[:, j * T:(j + 1) * T], ident[:, :])
                m.then_inc(misc_full, 1)

            pe.wait_ge(x_in, 16)
            for r in range(PREP_ROUNDS):
                prep_round(0, r, r + 1, SPLITS)

            def scores(q, par):
                st, c, g = q // PAIRS, (q // 2) % NT, q % 2
                for k in range(2):
                    h = 2 * g + k
                    m = nc.tensor.matmul(z[:, 2 * (q % 3) + k, 0:W], other_st[par][0:KR, h, c * T:c * T + P],
                                         self_st[par][0:KR, h, st * W:(st + 1) * W], start=True, stop=False,
                                         skip_group_check=True)
                m.then_inc(scored, 1)

            def masks(q, par):
                st, c, g = q // PAIRS, (q // 2) % NT, q % 2
                nc.tensor.matmul(z[:, 2 * (q % 3), 0:W], other_st[par][0:KR, 2 * g, c * T:c * T + P],
                                 self_st[par][0:KR, 2 * g, st * W:(st + 1) * W], start=False, stop=True,
                                 skip_group_check=True)
                for k in range(2):
                    for j in range(SJ):
                        m = nc.tensor.matmul(z[:, 2 * (q % 3) + k, j * T:(j + 1) * T],
                                             am1[(par * NS + st) % 2][:, j, c * T:c * T + P],
                                             shift[:, 2 * g + k, st * SJ + j, :], start=False, stop=True,
                                             skip_group_check=True)
                m.then_inc(masked, 1)

            def values(c, par, slot):
                for h in range(H):
                    m = nc.tensor.matmul(numer[h * OW:(h + 1) * OW, 0:W], vals[par][0:T, c, h, :],
                                         probs[0:T, slot, h, :], start=c == 0, stop=c == NT - 1,
                                         skip_group_check=True)
                m.then_inc(pv_done, 1)

            def large_scores(i, par):
                pe.wait_ge(expd, at(i, par, QB, 3))
                pe.sem_inc(gate, 1)
                with pe.Fori(0, NT) as t:
                    for h in range(H):
                        pe.wait_ge(big_read, at(i, par, MAXIMA, h) + t * H)
                        for k in range(NS):
                            m = nc.tensor.matmul(z[0:T, 3 * (h % 2) + k, 0:W],
                                                 self_st[par][0:KR, h, bass.ts(t, T)],
                                                 other_st[par][0:KR, h, k * W:(k + 1) * W], start=True, stop=True,
                                                 skip_group_check=True)
                        m.then_inc(big_scored, 1)
                pe.wait_ge(big_parts, at(i, par, PARTS, 3))
                nc.tensor.transpose(z[:, 0, 0:P], row_max[:, :], ident[:, :]).then_inc(big_turned, 1)
                pe.wait_ge(big_parts, at(i, par, PARTS, PARTS))

            pe.wait_ge(shift_ready, 1)
            with pe.Fori(0, B // 2) as i:
                for par in range(2):
                    pe.wait_ge(stacks_in, at(i, par, 16 * STACK_DMAS, 16 * STACK_DMAS))
                    pe.wait_ge(safe_ready, at(i, par, 1, 1))
                    pe.sem_inc(gate, 1)
                    small = pe.value_load(safe[par][0:1, 0:1], min_val=0, max_val=1)
                    with pe.If(small == 0):
                        large_scores(i, par)
                    with pe.Else():
                        pe.sem_inc(big_scored, MAXIMA)
                        pe.sem_inc(big_turned, 1)
                    prep, epilogues = 0, 0
                    for q in range(2):
                        pe.wait_ge(expd, at(i, par, QB, q + 1))
                        scores(q, par)
                    for q in range(QB):
                        st, c, g = q // PAIRS, (q // 2) % NT, q % 2
                        if q == 0:
                            pe.wait_ge(shift_in, at(i, par, 48, 48))
                            pe.wait_ge(shift_zeroed, at(i, par, 16, 16))
                        if q % PAIRS == 0:
                            pe.wait_ge(stage_free, at(i, par, NT, SJ + SJ * (st + 1)))
                        pe.wait_ge(leaky_act, at(i, par, QB, q + 1))
                        pe.wait_ge(leaky_dve, at(i, par, QB, q + 1))
                        masks(q, par)
                        if q + 2 < QB:
                            pe.wait_ge(expd, at(i, par, QB, q + 3))
                            scores(q + 2, par)
                        if g == 1 and q > 1:
                            t = q // 2 - 1
                            pe.wait_ge(expd, at(i, par, QB, q + 2))
                            if t % NT == 0:
                                pe.wait_ge(numer_free, at(i, par, NS, t // NT + 1))
                            values(t % NT, par, t % 3)
                        if q in PREP_AT:
                            if prep == 0:
                                pe.wait_ge(x_in, at(i, par, 16, 32))
                            prep_round(1 - par, prep, at(i, par, ROUNDS, PREP_ROUNDS + prep + epilogues + 1),
                                       at(i, par, SPLITS, 2 * SPLITS))
                            prep += 1
                        if q in OUT_AT:
                            pe.wait_ge(numer_free, at(i, par, NS, epilogues + 2))
                            out_round(at(i, par, ROUNDS, PREP_ROUNDS + prep + epilogues + 1))
                            epilogues += 1
                    pe.wait_ge(expd, at(i, par, QB, QB + 3))
                    values(NT - 1, par, (NS * NT - 1) % 3)
                    pe.wait_ge(numer_free, at(i, par, NS, NS + 1))
                    out_round(at(i, par, ROUNDS, PREP_ROUNDS + ROUNDS))

        @block.scalar
        def _(act):
            act.sem_inc(expd, 3)

            def leaky(q):
                bank = z[0:T, 2 * (q % 3), 0:W]
                nc.scalar.activation(bank, bank, ACT.Relu, scale=GAIN).then_inc(leaky_act, 1)

            with act.Fori(0, B // 2) as i:
                for par in range(2):
                    act.wait_ge(scored, at(i, par, QB, 1))
                    leaky(0)
                    for q in range(QB):
                        if q + 1 < QB:
                            act.wait_ge(scored, at(i, par, QB, q + 2))
                            leaky(q + 1)
                        act.wait_ge(masked, at(i, par, QB, q + 2))
                        if q % 2 == 0:
                            act.wait_ge(pv_done, at(i, par, NS * NT, q // 2 + 1))
                        nc.scalar.activation(probs[0:T, (q // 2) % 3, 2 * (q % 2):2 * (q % 2) + 2, :],
                                             z[0:T, 2 * (q % 3):2 * (q % 3) + 2, 0:W], ACT.Exp,
                                             scale=SCALE).then_inc(expd, 1)

        @block.vector
        def _(dve):
            dve.sem_inc(resid, 1)
            dve.sem_inc(big_read, 1)
            dve.sem_inc(misc_free, 1)
            dve.sem_inc(numer_free, 1)
            dve.sem_inc(pv_done, 3)

            def take(buf, r, n, flags):
                dve.wait_ge(misc_full, n)
                if r < XT_ROUNDS:
                    for k in range(2):
                        m = nc.vector.tensor_copy(
                            xT[:, 6 * T * r:6 * T * (r + 1)].rearrange("f (j k n) -> f j k n", k=2, n=T)[:, :, k, :],
                            misc[k * F:(k + 1) * F, 0:3 * T].rearrange("f (j n) -> f j n", n=T))
                    m.then_inc(misc_free, 1)
                elif r < PROJ_ROUNDS:
                    s0 = (r - XT_ROUNDS) * W
                    nc.vector.tensor_copy(proj[:, s0:s0 + W], misc[:, 0:W]).then_inc(misc_free, 1)
                elif r < VALS_ROUNDS:
                    c0 = 8 * (r - PROJ_ROUNDS)
                    c1 = min(c0 + 8, NT)
                    nc.vector.tensor_copy(vals[buf][0:T, c0:c1, :, 0:D],
                                          misc[0:T, 0:(c1 - c0) * HF].rearrange("p (c h d) -> p c h d", c=c1 - c0, h=H)
                                          ).then_inc(misc_free, 1)
                elif r == VALS_ROUNDS:
                    nc.vector.reduce_max(norm[0:T, 0:2 * H],
                                         misc[0:T, 0:NT * 2 * H].rearrange("p (c k) -> p k c", k=2 * H),
                                         axis=AX_X).then_inc(misc_free, 1)
                elif r == VALS_ROUNDS + 1:
                    nc.vector.reduce_max(norm_t[0:2 * H, 0:1], misc[0:2 * H, 0:P], axis=AX_X).then_inc(misc_free, 1)
                else:
                    nc.vector.reduce_max(flag_f[0:1, 0:1], misc[0:1, 0:H], axis=AX_X).then_inc(flag, 1)
                    nc.vector.reduce_max(flag_f[0:1, 1:2], misc[0:1, H:2 * H], axis=AX_X).then_inc(misc_free, 1)
                    dve.wait_ge(misc_free, n + 1)
                    dve.wait_ge(flag, flags + 1)
                    nc.vector.tensor_tensor(flag_f[0:1, 2:3], flag_f[0:1, 0:1], flag_f[0:1, 1:2],
                                            ALU.mult).then_inc(flag, 1)
                    dve.wait_ge(flag, flags + 2)
                    nc.vector.tensor_scalar(flag_f[0:1, 3:4], flag_f[0:1, 2:3], 1.0 / 16, SAFE * SAFE,
                                            ALU.mult, ALU.is_le).then_inc(flag, 1)
                    dve.wait_ge(flag, flags + 3)
                    nc.vector.tensor_copy(safe[buf][0:1, 0:1], flag_f[0:1, 3:4]).then_inc(safe_ready, 1)

            def large_scores(i, par):
                with dve.Fori(0, NT) as t:
                    dve.wait_ge(big_adj_in, at(i, par, 16 * NT, 16) + t * 16)
                    nc.vector.tensor_scalar(rest[0:T, :], rest[0:T, :], -1.0, BIG,
                                            ALU.add, ALU.mult).then_inc(big_max, 1)
                    dve.wait_ge(big_max, at(i, par, MAXIMA + NT, 1) + t * (H + 1))
                    for h in range(H):
                        dve.wait_ge(big_scored, at(i, par, MAXIMA, h + 1) + t * H)
                        nc.vector.tensor_tensor(proj[0:T, :].rearrange("p (k n) -> p k n", k=NS),
                                                z[0:T, 3 * (h % 2):3 * (h % 2) + 3, 0:W],
                                                rest[0:T, :].rearrange("p (k n) -> p k n", k=NS),
                                                ALU.add).then_inc(big_read, 1)
                        dve.wait_ge(big_read, at(i, par, MAXIMA, h + 2) + t * H)
                        nc.vector.reduce_max(row_max[0:T, bass.ds(h * NT + t, 1)], proj[0:T, :],
                                             axis=AX_X).then_inc(big_max, 1)
                mx, tmp = row_max[0:T, 0:MAXIMA], row_tmp[0:T, 0:MAXIMA]
                dve.wait_ge(big_max, at(i, par, MAXIMA + NT, MAXIMA + NT))
                nc.vector.tensor_scalar(tmp, mx, -BIG / 1024, None, ALU.is_gt).then_inc(big_parts, 1)
                dve.wait_ge(big_parts, at(i, par, PARTS, 1))
                nc.vector.scalar_tensor_tensor(tmp, mx, -1.0, tmp, ALU.mult, ALU.mult).then_inc(big_parts, 1)
                dve.wait_ge(big_parts, at(i, par, PARTS, 2))
                nc.vector.scalar_tensor_tensor(mx, tmp, 1.0 + GAIN, tmp, ALU.mult, ALU.min).then_inc(big_parts, 1)
                dve.wait_ge(big_turned, at(i, par, 1, 1))
                turned, left = z[0:MAXIMA, 0, 0:T], row_tmp[0:MAXIMA, 0:T]
                nc.vector.tensor_copy(max_part[0][:, :], turned).then_inc(big_parts, 1)
                dve.wait_ge(big_parts, at(i, par, PARTS, 4))
                nc.vector.tensor_tensor(left, turned, max_part[0][:, :], ALU.subtract).then_inc(big_parts, 1)
                dve.wait_ge(big_parts, at(i, par, PARTS, 5))
                nc.vector.tensor_copy(max_part[1][:, :], left).then_inc(big_parts, 1)
                dve.wait_ge(big_parts, at(i, par, PARTS, 6))
                nc.vector.tensor_tensor(max_part[2][:, :], left, max_part[1][:, :],
                                        ALU.subtract).then_inc(big_parts, 1)

            def leaky(q, i, par):
                bank = z[0:T, 2 * (q % 3) + 1, 0:W]
                dve.wait_ge(scored, at(i, par, QB, q + 1))
                nc.vector.tensor_scalar(relu_dve[0:T, q % 2, :], bank, 0.0, GAIN,
                                        ALU.max, ALU.mult).then_inc(half, 1)
                dve.wait_ge(half, at(i, par, QB, q + 1))
                nc.vector.tensor_tensor(bank, bank, relu_dve[0:T, q % 2, :],
                                        ALU.add).then_inc(leaky_dve, 1)

            def finish(step, st, i, par, misc_n):
                summed = misc[0:T, 0:SJ * P].rearrange("p (j c) -> p j c", c=OW)
                if step == 0:
                    dve.wait_ge(pv_done, at(i, par, NS * NT, (st + 1) * NT + 3))
                    nc.vector.tensor_copy(o_sb[:, :], numer[:, 0:W]).then_inc(numer_free, 1)
                elif step == 1:
                    dve.wait_ge(misc_full, misc_n)
                    nc.vector.tensor_scalar(den[0:T, :], summed[:, :, D], 1e-30, None, ALU.max).then_inc(epi, 1)
                elif step == 2:
                    dve.wait_ge(epi, at(i, par, 4 * NS, 4 * st + 1))
                    nc.vector.reciprocal(rden[0:T, :], den[0:T, :]).then_inc(epi, 1)
                elif step == 3:
                    dve.wait_ge(epi, at(i, par, 4 * NS, 4 * st + 2))
                    nc.vector.tensor_tensor(ob[0:T, :, :].rearrange("p j (h d) -> p (j h) d", d=D),
                                            summed[:, :, 0:D],
                                            rden[0:T, :].unsqueeze(2).broadcast_to([T, SJ * H, D]),
                                            ALU.mult).then_inc(misc_free, 1)
                elif step == 4:
                    dve.wait_ge(misc_free, misc_n + 1)
                    nc.vector.tensor_tensor(ob[0:T, :, :], ob[0:T, :, :],
                                            bias_rep[0:T, :].unsqueeze(1).broadcast_to([T, SJ, HF]),
                                            ALU.add).then_inc(epi, 1)
                elif step == 5:
                    dve.wait_ge(epi, at(i, par, 4 * NS, 4 * st + 3))
                    nc.vector.scalar_tensor_tensor(yb[0:T, :, :], ob[0:T, :, :], 0.0,
                                                   x_sb[par][0:T, st * SJ:(st + 1) * SJ, :], ALU.max,
                                                   ALU.add).then_inc(resid, 1)
                elif step == 6:
                    dve.wait_ge(resid, at(i, par, NS, st + 2))
                    nc.vector.reduce_sum(mean[0:T, :], yb[0:T, :, :], axis=AX_X).then_inc(epi, 1)
                elif step == 7:
                    dve.wait_ge(epi, at(i, par, 4 * NS, 4 * st + 4))
                    nc.vector.tensor_scalar(mean[0:T, :], mean[0:T, :], 1.0 / HF, None,
                                            ALU.mult).then_inc(mean_ready, 1)
                elif step == 8:
                    dve.wait_ge(squared, at(i, par, NS, st + 1))
                    nc.vector.reduce_sum(var[0:T, st * SJ:(st + 1) * SJ], sq[0:T, :, :],
                                         axis=AX_X).then_inc(newton, 1)

            def inverse_root(i, par):
                n = [NS]

                def before():
                    dve.wait_ge(newton, at(i, par, NEWTON, n[0]))
                    n[0] += 1
                v, y, t = var[0:T, :], rstd[0:T, :], nwt[0:T, :]
                before()
                nc.vector.tensor_scalar(v, v, 1.0 / HF, EPS, ALU.mult, ALU.add).then_inc(newton, 1)
                before()
                dve.wait_ge(normed, at(i, par, 1, 1))
                nc.vector.tensor_scalar(t.bitcast(I32), v.bitcast(I32), 1, None,
                                        ALU.logical_shift_right).then_inc(newton, 1)
                before()
                nc.vector.tensor_scalar(y.bitcast(I32), t.bitcast(I32), -1.0, float(0x5F3759DF),
                                        ALU.mult, ALU.add).then_inc(newton, 1)
                for step in range(ROOT_STEPS):
                    before()
                    nc.vector.tensor_tensor(t, y, y, ALU.mult).then_inc(newton, 1)
                    before()
                    nc.vector.scalar_tensor_tensor(t, t, -0.5, v, ALU.mult, ALU.mult).then_inc(newton, 1)
                    before()
                    nc.vector.scalar_tensor_tensor(y, t, 1.5, y, ALU.add, ALU.mult
                                                   ).then_inc(*((rstd_ready, 1) if step == ROOT_STEPS - 1
                                                                else (newton, 1)))
                assert n[0] == NEWTON + 1

            dve.wait_ge(consts, CONSTS)
            dve.wait_ge(pads, 4)
            for r in range(PREP_ROUNDS):
                take(0, r, r + 1, 0)
            with dve.Fori(0, B // 2) as i:
                for par in range(2):
                    dve.wait_ge(safe_ready, at(i, par, 1, 1))
                    dve.sem_inc(gate, 1)
                    small = dve.value_load(safe[par][0:1, 0:1], min_val=0, max_val=1)
                    with dve.If(small == 0):
                        large_scores(i, par)
                    with dve.Else():
                        dve.sem_inc(big_read, MAXIMA)
                        dve.sem_inc(big_max, MAXIMA + NT)
                        dve.sem_inc(big_parts, PARTS)
                    prep, epilogues = 0, 0
                    for q in range(QB):
                        leaky(q, i, par)
                        if q - 1 in PREP_AT:
                            take(1 - par, prep, at(i, par, ROUNDS, PREP_ROUNDS + prep + epilogues + 1),
                                 at(i, par, 3, 3))
                            prep += 1
                        if q - 2 in OUT_AT:
                            epilogues += 1
                            late = prep + epilogues
                        for step, dq in enumerate(FINISH_AFTER):
                            st = (q - dq) // PAIRS - 1
                            if q >= PAIRS + 1 and (q - dq) % PAIRS == 0 and 0 <= st < NS - 1:
                                finish(step, st, i, par,
                                       at(i, par, ROUNDS, PREP_ROUNDS + late) if step else None)
                    for step in range(9):
                        finish(step, NS - 1, i, par, at(i, par, ROUNDS, PREP_ROUNDS + ROUNDS))
                    inverse_root(i, par)


_INS = ["x", "adj", "L0_gnn_kernel", "L0_gnn_attention_kernel", "L0_gnn_attention_kernel_2", "L0_gnn_bias"]


def kernel(**inputs):
    import numpy as _np
    import concourse.bacc as _bacc
    from concourse import mybir as _mybir
    from concourse.bass_utils import run_bass_kernel_spmd as _run

    nc = _bacc.Bacc("TRN2", target_bir_lowering=False, num_devices=1)
    arrays, args = {}, []
    for name in _INS:
        a = _np.ascontiguousarray(inputs[name])
        arrays[f"in_{name}"] = a
        args.append(nc.dram_tensor(f"in_{name}", a.shape, _mybir.dt.from_np(a.dtype), kind="ExternalInput").ap())
    out = nc.dram_tensor("out", (B, N, F), F32, kind="ExternalOutput").ap()
    gat_layer(nc, *args, out)
    r = _run(nc, [arrays], core_ids=[0])
    return r.results[0]["out"]
```

```python
from contextlib import ExitStack

import concourse.bass as bass
from concourse import mybir

F32 = mybir.dt.float32
BF16 = mybir.dt.bfloat16
I32 = mybir.dt.int32
ALU = mybir.AluOpType
ACT = mybir.ActivationFunctionType
AX_X = mybir.AxisListType.X

P = 128
B, N, F, H, D = 8, 1500, 64, 4, 16
T = 125
NT = N // T
SJ = 4
W = SJ * T
NS = NT // SJ
NPAD = 1536
UNITS = H * NT
UB = NS * UNITS
BANKS = 6
LEAD = 4
HF = H * D
OW = 32
BIG = 2.0 ** 100
GAIN = 4.0
SCALE = 0.05
EPS = 1e-5
SELF_PART = (0, 0, 1, 1, 0, 2)
OTHER_PART = (0, 1, 0, 1, 2, 0)
KR = D * len(SELF_PART)
SAFE = 60.0

ROOT_STEPS = 3
ROOT = 3 + 3 * ROOT_STEPS
NEWTON = NS + ROOT - 1
SPLITS = 6
MAXIMA = NT * H
PARTS = 7
CONSTS = 13
STACK_DMAS = 2 * H * len(SELF_PART)
XT_ROUNDS = 2
PROJ_ROUNDS = XT_ROUNDS + NS
VALS_ROUNDS = PROJ_ROUNDS + 2
PREP_ROUNDS = VALS_ROUNDS + 3
ROUNDS = PREP_ROUNDS + NS
PREP_AT = [26, 30, 34, 38, 42, 64, 68, 78, 82, 88]
OUT_AT = 6
FINISH_AT = (3, 9, 13, 15, 17, 19, 21, 23, 29)
ROOT_AT = 33
_USES = [n for _, n in sorted([(u, n) for n, u in enumerate(PREP_AT)] + [(UNITS * k + OUT_AT, -1 - k) for k in range(NS)])]
PREP_PLACE = [1 + _USES.index(k) for k in range(PREP_ROUNDS)]
OUT_PLACE = [1 + _USES.index(-1 - k) for k in range(NS)]
OUT_PLACE_LAST = [1, 2, 3]


def gat_layer(nc, x, adj, w_feat, w_self, w_other, bias, out):
    with ExitStack() as ctx:
        def sb(name, shape, dt):
            return ctx.enter_context(nc.sbuf_tensor(name, shape, dt))

        def sem(name):
            return ctx.enter_context(nc.semaphore(name))

        w_proj = sb("w_proj", [F, 2 * HF], F32)
        w_val = sb("w_val", [F, HF], F32)
        bias_rep = sb("bias_rep", [P, HF], F32)
        ident = sb("ident", [P, P], F32)
        head_sum = sb("head_sum", [P, 2 * H], F32)
        x_sb = [sb(f"x_sb{p}", [P, NT, F], F32) for p in range(2)]
        xT = sb("xT", [F, N], F32)
        proj = sb("proj", [P, N], F32)
        rest = sb("rest", [P, N], F32)
        parts = [sb(f"part{k}", [P, N], BF16) for k in range(3)]
        self_st = [sb(f"self_st{p}", [KR, H, N], BF16) for p in range(2)]
        other_st = [sb(f"other_st{p}", [KR, H, NPAD], BF16) for p in range(2)]
        vals = [sb(f"vals{p}", [P, NT, H, OW], F32) for p in range(2)]
        stage = sb("stage", [P, SJ, N], F32)
        am1 = [sb(f"am1_{k}", [P, SJ, NPAD], BF16) for k in range(2)]
        shift = sb("shift", [P, H, NT, T], BF16)
        probs = sb("probs", [P, 3, H, W], F32)
        relu_dve = sb("relu_dve", [P, 2, W], F32)
        o_sb = sb("o_sb", [P, W], F32)
        den = sb("den", [P, SJ * H], F32)
        rden = sb("rden", [P, SJ * H], F32)
        ob = sb("ob", [P, SJ, HF], F32)
        yb = sb("yb", [P, SJ, HF], F32)
        sq = sb("sq", [P, SJ, HF], F32)
        mean = sb("mean", [P, SJ], F32)
        cent = [sb(f"cent{p}", [P, NT, HF], F32) for p in range(2)]
        var = sb("var", [P, NT], F32)
        rstd = sb("rstd", [P, NT], F32)
        nwt = sb("nwt", [P, NT], F32)

        norm = sb("norm", [P, P], F32)
        norm_t = sb("norm_t", [P, P], F32)
        flag_f = sb("flag_f", [P, 4], F32)
        safe = [sb(f"safe{p}", [1, 1], I32) for p in range(2)]
        row_max = sb("row_max", [P, P], F32)
        row_tmp = sb("row_tmp", [P, P], F32)
        max_part = [sb(f"max_part{k}", [MAXIMA, T], BF16) for k in range(3)]
        zero_row = sb("zero_row", [P, T], BF16)

        z = ctx.enter_context(nc.psum_tensor("z", [P, 6, 512], F32))
        numer = ctx.enter_context(nc.psum_tensor("numer", [P, 512], F32))
        misc = ctx.enter_context(nc.psum_tensor("misc", [P, 512], F32))

        weights_in = sem("weights_in")
        x_in = sem("x_in")
        stage_in = [sem(f"stage_in{j}") for j in range(SJ)]
        stage_free = sem("stage_free")
        consts = sem("consts")
        misc_full = sem("misc_full")
        misc_free = sem("misc_free")
        splits = sem("splits")
        stacks_in = sem("stacks_in")
        scored = sem("scored")
        half = sem("half")
        leaky_act = sem("leaky_act")
        leaky_dve = sem("leaky_dve")
        masked = sem("masked")
        expd = sem("expd")
        pv_done = sem("pv_done")
        numer_free = sem("numer_free")
        resid = sem("resid")
        squared = sem("squared")
        epi = sem("epi")
        mean_ready = sem("mean_ready")
        centered = sem("centered")
        newton = sem("newton")
        rstd_ready = sem("rstd_ready")
        normed = sem("normed")
        shift_ready = sem("shift_ready")
        pads = sem("pads")
        am1_init = sem("am1_init")
        flag = sem("flag")
        safe_ready = sem("safe_ready")
        big_adj_in = sem("big_adj_in")
        big_scored = sem("big_scored")
        big_read = sem("big_read")
        big_max = sem("big_max")
        big_turned = sem("big_turned")
        big_parts = sem("big_parts")
        shift_in = sem("shift_in")
        shift_zeroed = sem("shift_zeroed")
        gate = sem("gate")
        stored = [sem(f"stored{p}") for p in range(2)]

        block = ctx.enter_context(nc.Block())

        def at(b, per, n):
            return b * per + n

        def use(b, n):
            return b * ROUNDS + (PREP_ROUNDS - 1 + n)

        def batches(eng, batch):
            batch(0, 0, first=True)
            with eng.Fori(0, B // 2 - 1) as i:
                batch(2 * i + 1, 1)
                batch(2 * i + 2, 0)
            batch(B - 1, 1, last=True)

        @block.sync
        def _(sp):
            def load_x(b, buf):
                sp.dma_start(x_sb[buf][0:T, :, :],
                             x[b, :, :].rearrange("(j p) f -> p j f", p=T)).then_inc(x_in, 16)

            def load_adj(b, tile, j):
                sp.dma_start(stage[0:T, j, :], adj[b, tile * T:(tile + 1) * T, :]).then_inc(stage_in[j], 16)

            def stack(buf):
                for g in range(len(SELF_PART)):
                    rows = slice(g * D, (g + 1) * D)
                    for h in range(H):
                        sp.dma_start(self_st[buf][rows, h, :],
                                     parts[SELF_PART[g]][h * D:(h + 1) * D, :]).then_inc(stacks_in, 16)
                        sp.dma_start(other_st[buf][rows, h, 0:N],
                                     parts[OTHER_PART[g]][HF + h * D:HF + (h + 1) * D, :]).then_inc(stacks_in, 16)

            sp.sem_inc(shift_zeroed, 16)
            sp.sem_inc(stored[0], 16)
            sp.sem_inc(stored[1], 16)
            load_x(0, 0)
            sp.dma_start(w_proj[:, 0:HF].rearrange("f (h d) -> f h d", h=H),
                         w_self.rearrange("h f d -> f h d")).then_inc(weights_in, 16)
            sp.dma_start(w_proj[:, HF:2 * HF].rearrange("f (h d) -> f h d", h=H),
                         w_other.rearrange("h f d -> f h d")).then_inc(weights_in, 16)
            sp.dma_start(w_val[:, :].rearrange("f (h d) -> f h d", h=H),
                         w_feat.rearrange("h f d -> f h d")).then_inc(weights_in, 16)
            sp.dma_start(bias_rep[:, :],
                         bias.rearrange("a b h d -> (a b) (h d)").broadcast_to([P, HF])).then_inc(weights_in, 16)
            for j in range(SJ):
                load_adj(0, j, j)
            sp.wait_ge(splits, SPLITS - 1)
            sp.wait_ge(consts, CONSTS)
            stack(0)
            def shift_rows(k):
                return shift[T + k:T + k + 1, :, :, :].rearrange("p h j n -> p (h j) n")

            def large_scores(b):
                with sp.Fori(0, NT) as t:
                    sp.wait_ge(big_read, at(b, MAXIMA, 1) + t * H)
                    sp.dma_start(rest[0:T, :], adj[b, bass.ts(t, T), :]).then_inc(big_adj_in, 16)
                sp.wait_ge(big_parts, at(b, PARTS, PARTS))
                for k in range(3):
                    sp.dma_start(shift_rows(k), max_part[k][:, :]).then_inc(shift_in, 16)

            def store(b, par):
                sp.wait_ge(normed, at(b, 1, 2))
                sp.dma_start(out[b, :, :].rearrange("(j p) f -> p j f", p=T),
                             cent[par][0:T, :, :]).then_inc(stored[par], 16)

            def batch(b, par, first=False, last=False):
                sp.wait_ge(safe_ready, at(b, 1, 1))
                sp.sem_inc(gate, 1)
                small = sp.value_load(safe[par][0:1, 0:1], min_val=0, max_val=1)
                with sp.If(small == 0):
                    large_scores(b)
                with sp.Else():
                    sp.sem_inc(big_adj_in, 16 * NT)
                    sp.sem_inc(shift_in, 16 * 3)
                for st in range(NS):
                    if not (last and st == NS - 1):
                        for j in range(SJ):
                            sp.wait_ge(stage_free, at(b, NT, st * SJ + j + SJ + 1))
                            if st == NS - 1:
                                load_adj(b + 1, j, j)
                            else:
                                load_adj(b, (st + 1) * SJ + j, j)
                    if st == 1:
                        if not last:
                            sp.wait_ge(resid, at(b, NS, 1))
                            load_x(b + 1, 1 - par)
                            sp.wait_ge(splits, at(b, SPLITS, 2 * SPLITS - 1))
                            stack(1 - par)
                        if not first:
                            store(b - 1, 1 - par)
                if last:
                    store(b, par)
                else:
                    with sp.If(small == 0):
                        sp.wait_ge(masked, at(b, UB, UB + 1))
                        sp.dma_start(shift[T:P, :, :, :].rearrange("p h j n -> p (h j) n"),
                                     zero_row[0:3, :].unsqueeze(1).broadcast_to([3, MAXIMA, T])
                                     ).then_inc(shift_zeroed, 16)
                    with sp.Else():
                        sp.sem_inc(shift_zeroed, 16)

            batches(sp, batch)
            for p in range(2):
                sp.wait_ge(stored[p], 16 * (B // 2) + 16)

        @block.gpsimd
        def _(pool):
            pool.sem_inc(stage_free, SJ)
            pool.sem_inc(normed, 1)
            pool.memset(ident[:, :], 0.0).then_inc(consts, 1)
            pool.memset(head_sum[:, :], 1.0).then_inc(consts, 1)
            pool.memset(shift[:, :, :, :], 0.0).then_inc(consts, 1)
            for p in range(2):
                pool.memset(vals[p][:, :, :, :], 0.0).then_inc(consts, 1)
                pool.memset(other_st[p][:, :, N:NPAD], 0.0).then_inc(consts, 1)
            pool.memset(zero_row[:, :], 0.0).then_inc(consts, 1)
            pool.wait_ge(consts, 8)
            pool.affine_select(out=ident[:, :], in_=ident[:, :], compare_op=ALU.not_equal, fill=1.0, base=0,
                               pattern=[[-1, P]], channel_multiplier=1).then_inc(consts, 1)
            pool.affine_select(out=head_sum[:, :], in_=head_sum[:, :], compare_op=ALU.is_ge, fill=0.0, base=0,
                               pattern=[[-D, 2 * H]], channel_multiplier=1).then_inc(consts, 1)
            for p in range(2):
                pool.memset(vals[p][:, :, :, D:D + 1], 1.0).then_inc(consts, 1)
            pool.wait_ge(consts, 12)
            pool.affine_select(out=head_sum[:, :], in_=head_sum[:, :], compare_op=ALU.is_ge, fill=0.0, base=D - 1,
                               pattern=[[D, 2 * H]], channel_multiplier=-1).then_inc(consts, 1)
            pool.affine_select(out=shift[:, :, :, :].rearrange("p h j n -> p (h j) n"),
                               in_=shift[:, :, :, :].rearrange("p h j n -> p (h j) n"),
                               compare_op=ALU.not_equal, fill=BIG, base=0, pattern=[[0, H * NT], [-1, T]],
                               channel_multiplier=1).then_inc(shift_ready, 1)
            for m in (norm, norm_t, row_max, row_tmp):
                pool.memset(m[:, :], 0.0).then_inc(pads, 1)
            pool.memset(am1[0][:, :, :], 1.0).then_inc(am1_init, 1)
            pool.memset(am1[1][:, :, :], 1.0).then_inc(am1_init, 1)
            pool.wait_ge(am1_init, 2)

            def convert(buf, j):
                pool.sem_inc(gate, 1)
                pool.tensor_scalar(am1[buf][0:T, j, 0:N], stage[0:T, j, :], -1.0, 1.0,
                                   ALU.add, ALU.mult).then_inc(stage_free, 1)

            def split(done):
                pool.sem_inc(gate, 1)
                pool.tensor_scalar(parts[0][:, :], proj[:, :], 1.0, 0.0, ALU.mult, ALU.add).then_inc(splits, 1)
                pool.wait_ge(splits, done + 1)
                pool.tensor_tensor(rest[:, :], proj[:, :], parts[0][:, :], ALU.subtract).then_inc(splits, 1)
                pool.wait_ge(splits, done + 2)
                pool.sem_inc(gate, 1)
                pool.tensor_scalar(parts[1][:, :], rest[:, :], 1.0, 0.0, ALU.mult, ALU.add).then_inc(splits, 1)
                pool.wait_ge(splits, done + 3)
                pool.tensor_tensor(rest[:, :], rest[:, :], parts[1][:, :], ALU.subtract).then_inc(splits, 1)
                pool.wait_ge(splits, done + 4)
                pool.sem_inc(gate, 1)
                pool.tensor_scalar(parts[2][:, :], rest[:, :], 1.0, 0.0, ALU.mult, ALU.add).then_inc(splits, 1)
                pool.wait_ge(splits, done + 5)
                pool.tensor_tensor(rest[:, :], proj[:, :], proj[:, :], ALU.mult).then_inc(splits, 1)

            def center(b, par, st):
                buf = par if st >= 0 else 1 - par
                rows = cent[buf][0:T, st % NS * SJ:(st % NS + 1) * SJ, :]
                pool.wait_ge(mean_ready, at(b, NS, st + 1))
                if st == 0:
                    pool.wait_ge(stored[par], (b - par) * 8 + 16)
                pool.tensor_tensor(rows, yb[0:T, :, :], mean[0:T, :].unsqueeze(2).broadcast_to([T, SJ, HF]),
                                   ALU.subtract).then_inc(centered, 1)
                pool.wait_ge(centered, at(b, NS, st + 1))
                pool.tensor_tensor(sq[0:T, :, :], rows, rows, ALU.mult).then_inc(squared, 1)

            def scale_rows(b, par):
                pool.wait_ge(rstd_ready, at(b, 1, 1))
                pool.tensor_tensor(cent[par][0:T, :, :], cent[par][0:T, :, :],
                                   rstd[0:T, :].unsqueeze(2).broadcast_to([T, NT, HF]), ALU.mult).then_inc(normed, 1)

            pool.wait_ge(misc_free, 1 + PROJ_ROUNDS)
            split(0)
            for j in range(SJ):
                pool.wait_ge(stage_in[j], 16)
                convert(0, j)

            def batch(b, par, first=False, last=False):
                for st in range(NS):
                    if not (last and st == NS - 1):
                        pool.wait_ge(masked, at(b, UB, st * UNITS + 1))
                        for j in range(SJ):
                            pool.wait_ge(stage_in[j], at(b, 16 * NS, 16 * (st + 2)))
                            convert((par * NS + st + 1) % 2, j)
                    if not (first and st == 0):
                        center(b, par, st - 1)
                    if st == 0:
                        if not last:
                            pool.wait_ge(misc_free, use(b, PREP_PLACE[PROJ_ROUNDS - 1]) + 1)
                            pool.wait_ge(stacks_in, at(b, 16 * STACK_DMAS, 16 * STACK_DMAS))
                            split(at(b, SPLITS, SPLITS))
                        if not first:
                            scale_rows(b - 1, 1 - par)

            batches(pool, batch)
            center(B, 0, -1)
            scale_rows(B - 1, 1)

        @block.tensor
        def _(pe):
            pe.sem_inc(masked, 1)
            pe.wait_ge(consts, CONSTS)
            pe.wait_ge(weights_in, 64)

            def xT_round(buf, r, n):
                pe.wait_ge(misc_free, n)
                for k in range(3):
                    j = 6 * r + 2 * k
                    m = nc.tensor.transpose(misc[:, k * T:(k + 1) * T],
                                            x_sb[buf][0:T, j:j + 2, :].rearrange("p j f -> p (j f)"),
                                            ident[0:T, 0:T])
                m.then_inc(misc_full, 1)

            def proj_round(r, n):
                pe.wait_ge(misc_free, n)
                nc.tensor.matmul(misc[:, 0:W], w_proj[:, :], xT[:, r * W:(r + 1) * W],
                                 start=True, stop=True).then_inc(misc_full, 1)

            def vals_round(r, n):
                pe.wait_ge(misc_free, n)
                for c in range(8 * r, min(8 * r + 8, NT)):
                    m = nc.tensor.matmul(misc[0:T, (c - 8 * r) * HF:(c - 8 * r + 1) * HF], xT[:, c * T:(c + 1) * T],
                                         w_val[:, :], start=True, stop=True)
                m.then_inc(misc_full, 1)

            def norms_round(r, n, split_done):
                pe.wait_ge(misc_free, n)
                if r == 0:
                    pe.wait_ge(splits, split_done)
                    for c in range(NT):
                        m = nc.tensor.matmul(misc[0:T, c * 2 * H:(c + 1) * 2 * H], rest[:, c * T:(c + 1) * T],
                                             head_sum[:, :], start=True, stop=True)
                else:
                    m = nc.tensor.transpose(misc[:, 0:P], (norm if r == 1 else norm_t)[:, :], ident[:, :])
                m.then_inc(misc_full, 1)

            def prep_round(buf, r, n, split_done):
                if r < XT_ROUNDS:
                    xT_round(buf, r, n)
                elif r < PROJ_ROUNDS:
                    proj_round(r - XT_ROUNDS, n)
                elif r < VALS_ROUNDS:
                    vals_round(r - PROJ_ROUNDS, n)
                else:
                    norms_round(r - VALS_ROUNDS, n, split_done)

            def out_round(n):
                pe.wait_ge(misc_free, n)
                for j in range(SJ):
                    m = nc.tensor.transpose(misc[0:T, j * P:(j + 1) * P], o_sb[:, j * T:(j + 1) * T], ident[:, :])
                m.then_inc(misc_full, 1)

            pe.wait_ge(x_in, 16)
            for r in range(PREP_ROUNDS):
                prep_round(0, r, r + 1, SPLITS)

            def scores(u, b, par, again=False):
                st, c, h = u // UNITS, (u // H) % NT, u % H
                if not again:
                    pe.wait_ge(expd, at(b, UB, u + 1))
                m = nc.tensor.matmul(z[:, u % BANKS, 0:W], other_st[par][0:KR, h, c * T:c * T + P],
                                     self_st[par][0:KR, h, st * W:(st + 1) * W], start=not again, stop=again,
                                     skip_group_check=True)
                if not again:
                    m.then_inc(scored, 1)

            def masks(u, b, par):
                st, c, h = u // UNITS, (u // H) % NT, u % H
                for j in range(SJ):
                    m = nc.tensor.matmul(z[:, u % BANKS, j * T:(j + 1) * T],
                                         am1[(par * NS + st) % 2][:, j, c * T:c * T + P],
                                         shift[:, h, st * SJ + j, :], start=False, stop=True, skip_group_check=True)
                m.then_inc(masked, 1)

            def values(t, b, par):
                pe.wait_ge(expd, at(b, UB, H * (t + 1) + BANKS))
                if t % NT == 0:
                    pe.wait_ge(numer_free, at(b, NS, t // NT + 1))
                for h in range(H):
                    m = nc.tensor.matmul(numer[h * OW:(h + 1) * OW, 0:W], vals[par][0:T, t % NT, h, :],
                                         probs[0:T, t % 3, h, :], start=t % NT == 0, stop=t % NT == NT - 1,
                                         skip_group_check=True)
                m.then_inc(pv_done, 1)

            def large_scores(b, par):
                pe.wait_ge(expd, at(b, UB, BANKS))
                pe.sem_inc(gate, 1)
                with pe.Fori(0, NT) as t:
                    for h in range(H):
                        pe.wait_ge(big_read, at(b, MAXIMA, h) + t * H)
                        for k in range(NS):
                            m = nc.tensor.matmul(z[0:T, 3 * (h % 2) + k, 0:W],
                                                 self_st[par][0:KR, h, bass.ts(t, T)],
                                                 other_st[par][0:KR, h, k * W:(k + 1) * W], start=True, stop=True,
                                                 skip_group_check=True)
                        m.then_inc(big_scored, 1)
                pe.wait_ge(big_parts, at(b, PARTS, 3))
                nc.tensor.transpose(z[:, 0, 0:P], row_max[:, :], ident[:, :]).then_inc(big_turned, 1)
                pe.wait_ge(big_parts, at(b, PARTS, PARTS))

            def batch(b, par, first=False, last=False):
                pe.wait_ge(stacks_in, at(b, 16 * STACK_DMAS, 16 * STACK_DMAS))
                pe.wait_ge(safe_ready, at(b, 1, 1))
                pe.sem_inc(gate, 1)
                small = pe.value_load(safe[par][0:1, 0:1], min_val=0, max_val=1)
                with pe.If(small == 0):
                    large_scores(b, par)
                with pe.Else():
                    pe.sem_inc(big_scored, MAXIMA)
                    pe.sem_inc(big_turned, 1)
                for u in range(LEAD):
                    scores(u, b, par)
                for u in range(UB):
                    if u == 0:
                        pe.wait_ge(shift_in, at(b, 48, 48))
                        pe.wait_ge(shift_zeroed, at(b, 16, 16))
                    if u % UNITS == 0:
                        pe.wait_ge(stage_free, at(b, NT, SJ + SJ * (u // UNITS + 1)))
                    if u % 2 == 0:
                        pe.wait_ge(leaky_act, at(b, UB // 2, u // 2 + 1))
                        scores(u, b, par, again=True)
                    else:
                        pe.wait_ge(leaky_dve, at(b, UB // 2, u // 2 + 1))
                    masks(u, b, par)
                    if u + LEAD < UB:
                        scores(u + LEAD, b, par)
                    if u % H == 1:
                        if u > H:
                            values(u // H - 1, b, par)
                        elif not first:
                            values(NS * NT - 1, b - 1, 1 - par)
                    if u in PREP_AT and not last:
                        n = PREP_AT.index(u)
                        if n == 0:
                            pe.wait_ge(x_in, at(b, 16, 32))
                        prep_round(1 - par, n, use(b, PREP_PLACE[n]), at(b, SPLITS, 2 * SPLITS))
                    if u % UNITS == OUT_AT and not (first and u == OUT_AT):
                        k = u // UNITS
                        pe.wait_ge(numer_free, at(b, NS, k + 1))
                        out_round(use(b, (OUT_PLACE_LAST if last else OUT_PLACE)[k]))

            pe.wait_ge(shift_ready, 1)
            batches(pe, batch)
            values(NS * NT - 1, B - 1, 1)
            pe.wait_ge(numer_free, at(B, NS, 1))
            out_round(use(B - 1, NS + 1))

        @block.scalar
        def _(act):
            act.sem_inc(expd, BANKS)

            def relu(u, b):
                bank = z[0:T, u % BANKS, 0:W]
                act.wait_ge(scored, at(b, UB, u + 1))
                nc.scalar.activation(bank, bank, ACT.Relu, scale=GAIN).then_inc(leaky_act, 1)

            def batch(b, par, first=False, last=False):
                relu(0, b)
                for u in range(UB):
                    if u % 2 == 0 and u + 2 < UB:
                        relu(u + 2, b)
                    act.wait_ge(masked, at(b, UB, u + 2))
                    if u % H == 0:
                        act.wait_ge(pv_done, at(b, NS * NT, u // H + 1))
                    nc.scalar.activation(probs[0:T, (u // H) % 3, u % H, :], z[0:T, u % BANKS, 0:W], ACT.Exp,
                                         scale=SCALE).then_inc(expd, 1)

            batches(act, batch)

        @block.vector
        def _(dve):
            dve.sem_inc(resid, 1)
            dve.sem_inc(big_read, 1)
            dve.sem_inc(misc_free, 1)
            dve.sem_inc(numer_free, 1)
            dve.sem_inc(pv_done, 3)

            def take(buf, r, n, flags):
                dve.wait_ge(misc_full, n)
                if r < XT_ROUNDS:
                    for k in range(2):
                        m = nc.vector.tensor_copy(
                            xT[:, 6 * T * r:6 * T * (r + 1)].rearrange("f (j k n) -> f j k n", k=2, n=T)[:, :, k, :],
                            misc[k * F:(k + 1) * F, 0:3 * T].rearrange("f (j n) -> f j n", n=T))
                    m.then_inc(misc_free, 1)
                elif r < PROJ_ROUNDS:
                    s0 = (r - XT_ROUNDS) * W
                    nc.vector.tensor_copy(proj[:, s0:s0 + W], misc[:, 0:W]).then_inc(misc_free, 1)
                elif r < VALS_ROUNDS:
                    c0 = 8 * (r - PROJ_ROUNDS)
                    c1 = min(c0 + 8, NT)
                    nc.vector.tensor_copy(vals[buf][0:T, c0:c1, :, 0:D],
                                          misc[0:T, 0:(c1 - c0) * HF].rearrange("p (c h d) -> p c h d", c=c1 - c0, h=H)
                                          ).then_inc(misc_free, 1)
                elif r == VALS_ROUNDS:
                    nc.vector.reduce_max(norm[0:T, 0:2 * H],
                                         misc[0:T, 0:NT * 2 * H].rearrange("p (c k) -> p k c", k=2 * H),
                                         axis=AX_X).then_inc(misc_free, 1)
                elif r == VALS_ROUNDS + 1:
                    nc.vector.reduce_max(norm_t[0:2 * H, 0:1], misc[0:2 * H, 0:P], axis=AX_X).then_inc(misc_free, 1)
                else:
                    nc.vector.reduce_max(flag_f[0:1, 0:1], misc[0:1, 0:H], axis=AX_X).then_inc(flag, 1)
                    nc.vector.reduce_max(flag_f[0:1, 1:2], misc[0:1, H:2 * H], axis=AX_X).then_inc(misc_free, 1)
                    dve.wait_ge(misc_free, n + 1)
                    dve.wait_ge(flag, flags + 1)
                    nc.vector.tensor_tensor(flag_f[0:1, 2:3], flag_f[0:1, 0:1], flag_f[0:1, 1:2],
                                            ALU.mult).then_inc(flag, 1)
                    dve.wait_ge(flag, flags + 2)
                    nc.vector.tensor_scalar(flag_f[0:1, 3:4], flag_f[0:1, 2:3], 1.0 / 16, SAFE * SAFE,
                                            ALU.mult, ALU.is_le).then_inc(flag, 1)
                    dve.wait_ge(flag, flags + 3)
                    nc.vector.tensor_copy(safe[buf][0:1, 0:1], flag_f[0:1, 3:4]).then_inc(safe_ready, 1)

            def large_scores(b):
                with dve.Fori(0, NT) as t:
                    dve.wait_ge(big_adj_in, at(b, 16 * NT, 16) + t * 16)
                    nc.vector.tensor_scalar(rest[0:T, :], rest[0:T, :], -1.0, BIG,
                                            ALU.add, ALU.mult).then_inc(big_max, 1)
                    for h in range(H):
                        dve.wait_ge(big_max, at(b, MAXIMA + NT, h + 1) + t * (H + 1))
                        dve.wait_ge(big_scored, at(b, MAXIMA, h + 1) + t * H)
                        nc.vector.tensor_tensor(proj[0:T, :].rearrange("p (k n) -> p k n", k=NS),
                                                z[0:T, 3 * (h % 2):3 * (h % 2) + 3, 0:W],
                                                rest[0:T, :].rearrange("p (k n) -> p k n", k=NS),
                                                ALU.add).then_inc(big_read, 1)
                        dve.wait_ge(big_read, at(b, MAXIMA, h + 2) + t * H)
                        nc.vector.reduce_max(row_max[0:T, bass.ds(h * NT + t, 1)], proj[0:T, :],
                                             axis=AX_X).then_inc(big_max, 1)
                mx, tmp = row_max[0:T, 0:MAXIMA], row_tmp[0:T, 0:MAXIMA]
                dve.wait_ge(big_max, at(b, MAXIMA + NT, MAXIMA + NT))
                nc.vector.tensor_scalar(tmp, mx, -BIG / 1024, None, ALU.is_gt).then_inc(big_parts, 1)
                dve.wait_ge(big_parts, at(b, PARTS, 1))
                nc.vector.scalar_tensor_tensor(tmp, mx, -1.0, tmp, ALU.mult, ALU.mult).then_inc(big_parts, 1)
                dve.wait_ge(big_parts, at(b, PARTS, 2))
                nc.vector.scalar_tensor_tensor(mx, tmp, 1.0 + GAIN, tmp, ALU.mult, ALU.min).then_inc(big_parts, 1)
                dve.wait_ge(big_turned, at(b, 1, 1))
                turned, left = z[0:MAXIMA, 0, 0:T], row_tmp[0:MAXIMA, 0:T]
                nc.vector.tensor_copy(max_part[0][:, :], turned).then_inc(big_parts, 1)
                dve.wait_ge(big_parts, at(b, PARTS, 4))
                nc.vector.tensor_tensor(left, turned, max_part[0][:, :], ALU.subtract).then_inc(big_parts, 1)
                dve.wait_ge(big_parts, at(b, PARTS, 5))
                nc.vector.tensor_copy(max_part[1][:, :], left).then_inc(big_parts, 1)
                dve.wait_ge(big_parts, at(b, PARTS, 6))
                nc.vector.tensor_tensor(max_part[2][:, :], left, max_part[1][:, :],
                                        ALU.subtract).then_inc(big_parts, 1)

            def leaky(u, b):
                bank, v = z[0:T, u % BANKS, 0:W], u // 2
                dve.wait_ge(scored, at(b, UB, u + 1))
                nc.vector.tensor_scalar(relu_dve[0:T, v % 2, :], bank, 0.0, GAIN,
                                        ALU.max, ALU.mult).then_inc(half, 1)
                dve.wait_ge(half, at(b, UB // 2, v + 1))
                nc.vector.tensor_tensor(bank, bank, relu_dve[0:T, v % 2, :], ALU.add).then_inc(leaky_dve, 1)

            def finish(step, st, b, par, misc_n):
                buf, t0 = par if st >= 0 else 1 - par, st % NS * SJ
                summed = misc[0:T, 0:SJ * P].rearrange("p (j c) -> p j c", c=OW)
                if step == 0:
                    dve.wait_ge(pv_done, at(b, NS * NT, (st + 1) * NT + 3))
                    nc.vector.tensor_copy(o_sb[:, :], numer[:, 0:W]).then_inc(numer_free, 1)
                elif step == 1:
                    dve.wait_ge(misc_full, misc_n)
                    nc.vector.tensor_scalar(den[0:T, :], summed[:, :, D], 1e-30, None, ALU.max).then_inc(epi, 1)
                elif step == 2:
                    dve.wait_ge(epi, at(b, 4 * NS, 4 * st + 1))
                    nc.vector.reciprocal(rden[0:T, :], den[0:T, :]).then_inc(epi, 1)
                elif step == 3:
                    dve.wait_ge(epi, at(b, 4 * NS, 4 * st + 2))
                    nc.vector.tensor_tensor(ob[0:T, :, :].rearrange("p j (h d) -> p (j h) d", d=D),
                                            summed[:, :, 0:D],
                                            rden[0:T, :].unsqueeze(2).broadcast_to([T, SJ * H, D]),
                                            ALU.mult).then_inc(misc_free, 1)
                elif step == 4:
                    dve.wait_ge(misc_free, misc_n + 1)
                    nc.vector.tensor_tensor(ob[0:T, :, :], ob[0:T, :, :],
                                            bias_rep[0:T, :].unsqueeze(1).broadcast_to([T, SJ, HF]),
                                            ALU.add).then_inc(epi, 1)
                elif step == 5:
                    dve.wait_ge(epi, at(b, 4 * NS, 4 * st + 3))
                    nc.vector.scalar_tensor_tensor(yb[0:T, :, :], ob[0:T, :, :], 0.0,
                                                   x_sb[buf][0:T, t0:t0 + SJ, :], ALU.max,
                                                   ALU.add).then_inc(resid, 1)
                elif step == 6:
                    dve.wait_ge(resid, at(b, NS, st + 2))
                    nc.vector.reduce_sum(mean[0:T, :], yb[0:T, :, :], axis=AX_X).then_inc(epi, 1)
                elif step == 7:
                    dve.wait_ge(epi, at(b, 4 * NS, 4 * st + 4))
                    nc.vector.tensor_scalar(mean[0:T, :], mean[0:T, :], 1.0 / HF, None,
                                            ALU.mult).then_inc(mean_ready, 1)
                elif step == 8:
                    dve.wait_ge(squared, at(b, NS, st + 1))
                    nc.vector.reduce_sum(var[0:T, t0:t0 + SJ], sq[0:T, :, :],
                                         axis=AX_X).then_inc(newton, 1)

            def inverse_root(step, b):
                v, y, t = var[0:T, :], rstd[0:T, :], nwt[0:T, :]
                dve.wait_ge(newton, at(b, NEWTON, NS + step))
                if step == 0:
                    nc.vector.tensor_scalar(v, v, 1.0 / HF, EPS, ALU.mult, ALU.add).then_inc(newton, 1)
                elif step == 1:
                    nc.vector.tensor_scalar(t.bitcast(I32), v.bitcast(I32), 1, None,
                                            ALU.logical_shift_right).then_inc(newton, 1)
                elif step == 2:
                    dve.wait_ge(normed, at(b, 1, 1))
                    nc.vector.tensor_scalar(y.bitcast(I32), t.bitcast(I32), -1.0, float(0x5F3759DF),
                                            ALU.mult, ALU.add).then_inc(newton, 1)
                elif step % 3 == 0:
                    nc.vector.tensor_tensor(t, y, y, ALU.mult).then_inc(newton, 1)
                elif step % 3 == 1:
                    nc.vector.scalar_tensor_tensor(t, t, -0.5, v, ALU.mult, ALU.mult).then_inc(newton, 1)
                else:
                    nc.vector.scalar_tensor_tensor(y, t, 1.5, y, ALU.add, ALU.mult
                                                   ).then_inc(rstd_ready if step == ROOT - 1 else newton, 1)

            dve.wait_ge(consts, CONSTS)
            dve.wait_ge(pads, 4)
            for r in range(PREP_ROUNDS):
                take(0, r, r + 1, 0)
            def batch(b, par, first=False, last=False):
                dve.wait_ge(safe_ready, at(b, 1, 1))
                dve.sem_inc(gate, 1)
                small = dve.value_load(safe[par][0:1, 0:1], min_val=0, max_val=1)
                with dve.If(small == 0):
                    large_scores(b)
                with dve.Else():
                    dve.sem_inc(big_read, MAXIMA)
                    dve.sem_inc(big_max, MAXIMA + NT)
                    dve.sem_inc(big_parts, PARTS)
                for u in range(1, UB, 2):
                    leaky(u, b)
                    if u - 3 in PREP_AT and not last:
                        n = PREP_AT.index(u - 3)
                        take(1 - par, n, use(b, PREP_PLACE[n]), at(b, 3, 3))
                    k = u // UNITS
                    if u % UNITS in FINISH_AT and not (first and k == 0):
                        finish(FINISH_AT.index(u % UNITS), k - 1, b, par,
                               use(b, (OUT_PLACE_LAST if last else OUT_PLACE)[k]))
                    if u - ROOT_AT in range(0, 2 * ROOT, 2) and not first:
                        inverse_root((u - ROOT_AT) // 2, b - 1)

            batches(dve, batch)
            for step in range(len(FINISH_AT)):
                finish(step, -1, B, 0, use(B - 1, NS + 1))
            for step in range(ROOT):
                inverse_root(step, B - 1)


_INS = ["x", "adj", "L0_gnn_kernel", "L0_gnn_attention_kernel", "L0_gnn_attention_kernel_2", "L0_gnn_bias"]


def kernel(**inputs):
    import numpy as _np
    import concourse.bacc as _bacc
    from concourse import mybir as _mybir
    from concourse.bass_utils import run_bass_kernel_spmd as _run

    nc = _bacc.Bacc("TRN2", target_bir_lowering=False, num_devices=1)
    arrays, args = {}, []
    for name in _INS:
        a = _np.ascontiguousarray(inputs[name])
        arrays[f"in_{name}"] = a
        args.append(nc.dram_tensor(f"in_{name}", a.shape, _mybir.dt.from_np(a.dtype), kind="ExternalInput").ap())
    out = nc.dram_tensor("out", (B, N, F), F32, kind="ExternalOutput").ap()
    gat_layer(nc, *args, out)
    r = _run(nc, [arrays], core_ids=[0])
    return r.results[0]["out"]
```

```python
from contextlib import ExitStack

import concourse.bass as bass
from concourse import mybir

F32 = mybir.dt.float32
BF16 = mybir.dt.bfloat16
I32 = mybir.dt.int32
ALU = mybir.AluOpType
ACT = mybir.ActivationFunctionType
AX_X = mybir.AxisListType.X

P = 128
B, N, F, H, D = 8, 1500, 64, 4, 16
T = 125
NT = N // T
SJ = 4
W = SJ * T
NS = NT // SJ
NPAD = 1536
UNITS = H * NT
UB = NS * UNITS
BANKS = 6
PROBS = 4
LOWS = 3
LEAKS = 3
PART_DMAS = 3
VALUES_LAG = 12
KINDS = "adeadaed"
LIFT_LAG = 2
RELU_LEAD = 2
COMBINE_LAG = 4
HF = H * D
OW = 32
BIG = 2.0 ** 100
GAIN = 4.0
LOW = 0.05
HIGH = 0.25
EPS = 1e-5
SELF_PART = (0, 0, 1, 1, 0, 2)
OTHER_PART = (0, 1, 0, 1, 2, 0)
KR = D * len(SELF_PART)
SAFE = 60.0

ROOT_STEPS = 3
ROOT = 3 + 3 * ROOT_STEPS
NEWTON = NS + ROOT - 1
SPLITS = 6 * NS
MAXIMA = NT * H
PARTS = 7
CONSTS = 10
STACK_DMAS = 2 * len(SELF_PART)
XT_ROUNDS = 2
PROJ_ROUNDS = XT_ROUNDS + NS
VALS_ROUNDS = PROJ_ROUNDS + 2
PREP_ROUNDS = VALS_ROUNDS + 2
ROUNDS = PREP_ROUNDS + NS
PREP_AT = [36, 41, 46, 51, 56, 73, 78, 86, 90]
TAKE_LAG = 2
OUT_AT = 14
FINISH_AT = (7, 17, 19, 21, 23, 25, 27, 29, 39)
ROOT_AT = 63
_USES = [n for _, n in sorted([(u, n) for n, u in enumerate(PREP_AT)]
                              + [(UNITS * k + OUT_AT, -1 - k) for k in range(NS)])]
PREP_PLACE = [1 + _USES.index(k) for k in range(PREP_ROUNDS)]
OUT_PLACE = [1 + _USES.index(-1 - k) for k in range(NS)]
OUT_PLACE_LAST = [1, 2, 3]


def kind(u):
    return KINDS[u % len(KINDS)]


def nth(kinds, u):
    return sum(kind(v) in kinds for v in range(u + 1))


D_PLACES = [u for u in range(UB) if kind(u) == "d"]
A_UNITS, D_UNITS, E_UNITS = (nth(k, UB - 1) for k in "ade")
assert D_UNITS % LEAKS == 0 and E_UNITS % LOWS == 0 and (NS * NT) % PROBS == 0 and UB % BANKS == 0


def gat_layer(nc, x, adj, w_feat, w_self, w_other, bias, out):
    with ExitStack() as ctx:
        def sb(name, shape, dt):
            return ctx.enter_context(nc.sbuf_tensor(name, shape, dt))

        def sem(name):
            return ctx.enter_context(nc.semaphore(name))

        w_proj = sb("w_proj", [F, 2 * HF], F32)
        w_val = sb("w_val", [F, HF], F32)
        bias_rep = sb("bias_rep", [P, HF], F32)
        ident = sb("ident", [P, P], F32)
        head_sum = sb("head_sum", [P, OW], F32)
        x_sb = [sb(f"x_sb{p}", [P, NT, F], F32) for p in range(2)]
        xT = sb("xT", [F, N], F32)
        proj = sb("proj", [P, N], F32)
        rest = sb("rest", [P, N], F32)
        parts = [sb(f"part{k}", [P, N], BF16) for k in range(3)]
        self_st = [sb(f"self_st{p}", [KR + 3, H, N], BF16) for p in range(2)]
        other_st = [sb(f"other_st{p}", [KR, H, NPAD], BF16) for p in range(2)]
        vals = [sb(f"vals{p}", [P, NT, H, OW], F32) for p in range(2)]
        edges = [sb(f"edges{k}", [P, SJ, NPAD], F32) for k in range(2)]
        edge_w = sb("edge_w", [P, T], BF16)
        probs = sb("probs", [P, PROBS, H, W], F32)
        low = sb("low", [P, LOWS, W], F32)
        leak = sb("leak", [P, LEAKS, W], F32)
        o_sb = sb("o_sb", [P, W], F32)
        den = sb("den", [P, SJ * H], F32)
        rden = sb("rden", [P, SJ * H], F32)
        ob = sb("ob", [P, SJ, HF], F32)
        yb = sb("yb", [P, SJ, HF], F32)
        sq = sb("sq", [P, SJ, HF], F32)
        mean = sb("mean", [P, SJ], F32)
        cent = [sb(f"cent{p}", [P, NT, HF], F32) for p in range(2)]
        var = sb("var", [P, NT], F32)
        rstd = sb("rstd", [P, NT], F32)
        nwt = sb("nwt", [P, NT], F32)

        norm = sb("norm", [P, P], F32)
        flag_f = sb("flag_f", [P, 2 * H + 4], F32)
        safe = [sb(f"safe{p}", [1, 1], I32) for p in range(2)]
        row_max = sb("row_max", [P, P], F32)
        row_tmp = sb("row_tmp", [P, P], F32)
        max_part = [sb(f"max_part{k}", [MAXIMA, T], BF16) for k in range(3)]
        shift_w = sb("shift_w", [KR + 3, P], BF16)
        parts_dram = nc.dram_tensor("parts_dram", (3, P, N), BF16).ap()

        z = ctx.enter_context(nc.psum_tensor("z", [P, BANKS, 512], F32))
        numer = ctx.enter_context(nc.psum_tensor("numer", [P, 512], F32))
        misc = ctx.enter_context(nc.psum_tensor("misc", [P, 512], F32))

        weights_in = sem("weights_in")
        x_in = sem("x_in")
        edges_in = [sem(f"edges_in{k}") for k in range(2)]
        consts = sem("consts")
        misc_full = sem("misc_full")
        misc_free = sem("misc_free")
        splits = sem("splits")
        stacks_in = sem("stacks_in")
        scored = sem("scored")
        half = sem("half")
        leaky_act = sem("leaky_act")
        leaky_dve = sem("leaky_dve")
        relu_large = sem("relu_large")
        lifted = sem("lifted")
        lifted_large = sem("lifted_large")
        combined = sem("combined")
        expd = sem("expd")
        pv_done = sem("pv_done")
        numer_free = sem("numer_free")
        resid = sem("resid")
        squared = sem("squared")
        epi = sem("epi")
        mean_ready = sem("mean_ready")
        centered = sem("centered")
        newton = sem("newton")
        rstd_ready = sem("rstd_ready")
        normed = sem("normed")
        pads = sem("pads")
        ident_ready = sem("ident_ready")
        vals_init = sem("vals_init")
        edges_init = [sem(f"edges_init{k}") for k in range(2)]
        parts_out = sem("parts_out")
        flag = sem("flag")
        safe_ready = sem("safe_ready")
        big_adj_in = sem("big_adj_in")
        big_scored = sem("big_scored")
        big_read = sem("big_read")
        big_max = sem("big_max")
        big_turned = sem("big_turned")
        big_parts = sem("big_parts")
        shift_in = sem("shift_in")
        gate = sem("gate")
        stored = [sem(f"stored{p}") for p in range(2)]

        block = ctx.enter_context(nc.Block())

        def at(b, per, n):
            return b * per + n

        def edges_count(b, par, st):
            return (b - par) * (16 * NS // 2) + 16 * ((par * NS + st) // 2 + 1)

        def use(b, n):
            return b * ROUNDS + (PREP_ROUNDS - 1 + n)

        def batches(eng, batch):
            batch(0, 0, first=True)
            with eng.Fori(0, B // 2 - 1) as i:
                batch(2 * i + 1, 1)
                batch(2 * i + 2, 0)
            batch(B - 1, 1, last=True)

        @block.sync
        def _(sp):
            def load_x(b, buf):
                sp.dma_start(x_sb[buf][0:T, :, :],
                             x[b, :, :].rearrange("(j p) f -> p j f", p=T)).then_inc(x_in, 16)

            def load_edges(b, par, st):
                sp.dma_start(edges[(par * NS + st) % 2][0:T, :, 0:N],
                             adj[b, st * W:(st + 1) * W, :].rearrange("(j p) n -> p j n", p=T)
                             ).then_inc(edges_in[(par * NS + st) % 2], 16)

            def stack(buf, k, done, written):
                sp.wait_ge(splits, done + (NS, 4 * NS, 6 * NS)[k])
                sp.dma_start(parts_dram[k, :, :], parts[k][:, :]).then_inc(parts_out, 16)
                sp.wait_ge(parts_out, written + 16 * (k + 1))
                for g in range(len(SELF_PART)):
                    rows = slice(g * D, (g + 1) * D)
                    if SELF_PART[g] == k:
                        sp.dma_start(self_st[buf][rows, :, :],
                                     parts_dram[k, 0:HF, :].rearrange("(h d) n -> d h n", h=H)).then_inc(stacks_in, 16)
                    if OTHER_PART[g] == k:
                        sp.dma_start(other_st[buf][rows, :, 0:N],
                                     parts_dram[k, HF:2 * HF, :].rearrange("(h d) n -> d h n", h=H)
                                     ).then_inc(stacks_in, 16)

            sp.sem_inc(stored[0], 16)
            sp.sem_inc(stored[1], 16)
            load_x(0, 0)
            sp.dma_start(w_proj[:, 0:HF].rearrange("f (h d) -> f h d", h=H),
                         w_self.rearrange("h f d -> f h d")).then_inc(weights_in, 16)
            sp.dma_start(w_proj[:, HF:2 * HF].rearrange("f (h d) -> f h d", h=H),
                         w_other.rearrange("h f d -> f h d")).then_inc(weights_in, 16)
            sp.dma_start(w_val[:, :].rearrange("f (h d) -> f h d", h=H),
                         w_feat.rearrange("h f d -> f h d")).then_inc(weights_in, 16)
            sp.dma_start(bias_rep[:, :],
                         bias.rearrange("a b h d -> (a b) (h d)").broadcast_to([P, HF])).then_inc(weights_in, 16)
            sp.wait_ge(edges_init[0], 1)
            load_edges(0, 0, 0)
            for k in range(3):
                stack(0, k, 0, 0)

            def large_scores(b, par):
                with sp.Fori(0, NT) as t:
                    sp.wait_ge(big_read, at(b, MAXIMA, 2) + t * H)
                    sp.dma_start(rest[0:T, :], adj[b, bass.ts(t, T), :]).then_inc(big_adj_in, 16)
                sp.wait_ge(big_parts, at(b, PARTS, PARTS))
                for k in range(3):
                    sp.dma_start(self_st[par][KR + k:KR + k + 1, :, :].rearrange("p h (j n) -> p (h j) n", n=T),
                                 max_part[k][:, :]).then_inc(shift_in, 16)

            def store(b, par):
                sp.wait_ge(normed, at(b, 1, 2))
                sp.dma_start(out[b, :, :].rearrange("(j p) f -> p j f", p=T),
                             cent[par][0:T, :, :]).then_inc(stored[par], 16)

            def batch(b, par, first=False, last=False):
                sp.wait_ge(safe_ready, at(b, 1, 1))
                sp.sem_inc(gate, 1)
                small = sp.value_load(safe[par][0:1, 0:1], min_val=0, max_val=1)
                with sp.If(small == 0):
                    large_scores(b, par)
                with sp.Else():
                    sp.sem_inc(big_adj_in, 16 * NT)
                    sp.sem_inc(shift_in, 16 * 3)
                for st in range(NS):
                    if first and st == 0:
                        sp.wait_ge(edges_init[1], 1)
                    if not (last and st == NS - 1):
                        sp.wait_ge(expd, at(b, UB, st * UNITS + BANKS))
                        if st == NS - 1:
                            load_edges(b + 1, 1 - par, 0)
                        else:
                            load_edges(b, par, st + 1)
                    if st == 0 and not last:
                        sp.wait_ge(resid, at(b, NS, 1))
                        load_x(b + 1, 1 - par)
                        stack(1 - par, 0, at(b, SPLITS, SPLITS), at(b, 16 * PART_DMAS, 16 * PART_DMAS))
                    if st == 1 and not last:
                        stack(1 - par, 1, at(b, SPLITS, SPLITS), at(b, 16 * PART_DMAS, 16 * PART_DMAS))
                if not last:
                    stack(1 - par, 2, at(b, SPLITS, SPLITS), at(b, 16 * PART_DMAS, 16 * PART_DMAS))
                if not first:
                    store(b - 1, 1 - par)
                if last:
                    store(b, par)

            batches(sp, batch)
            for p in range(2):
                sp.wait_ge(stored[p], 16 * (B // 2) + 16)

        @block.gpsimd
        def _(pool):
            pool.sem_inc(normed, 1)
            pool.memset(ident[:, :], 0.0).then_inc(consts, 1)
            pool.memset(head_sum[:, :], 1.0).then_inc(consts, 1)
            pool.wait_ge(consts, 2)
            pool.affine_select(out=ident[:, :], in_=ident[:, :], compare_op=ALU.not_equal, fill=1.0, base=0,
                               pattern=[[-1, P]], channel_multiplier=1).then_inc(ident_ready, 1)
            pool.affine_select(out=head_sum[:, :], in_=head_sum[:, :], compare_op=ALU.is_ge, fill=0.0, base=0,
                               pattern=[[-D, OW]], channel_multiplier=1).then_inc(consts, 1)
            pool.memset(edge_w[:, :], 0.0).then_inc(consts, 1)
            pool.wait_ge(consts, 4)
            pool.affine_select(out=head_sum[:, :], in_=head_sum[:, :], compare_op=ALU.is_ge, fill=0.0, base=D - 1,
                               pattern=[[D, OW]], channel_multiplier=-1).then_inc(consts, 1)
            pool.affine_select(out=edge_w[:, :], in_=edge_w[:, :], compare_op=ALU.not_equal, fill=BIG, base=0,
                               pattern=[[-1, T]], channel_multiplier=1).then_inc(consts, 1)
            pool.wait_ge(consts, 6)
            pool.affine_select(out=edge_w[:, :], in_=edge_w[:, :], compare_op=ALU.not_equal, fill=-BIG, base=-T,
                               pattern=[[0, T]], channel_multiplier=1).then_inc(consts, 1)
            for p in range(2):
                pool.memset(other_st[p][:, :, N:NPAD], 0.0).then_inc(consts, 1)
            for m in (norm, row_max, row_tmp):
                pool.memset(m[:, :], 0.0).then_inc(pads, 1)
            pool.memset(shift_w[:, :], 1.0).then_inc(consts, 1)
            for p in range(2):
                pool.memset(vals[p][:, :, :, :], 0.0).then_inc(vals_init, 1)
                pool.memset(edges[p][:, :, :], 1.0).then_inc(edges_init[p], 1)
                pool.wait_ge(vals_init, 2 * p + 1)
                pool.memset(vals[p][:, :, :, D:D + 1], 1.0).then_inc(vals_init, 1)

            def split(k, n):
                cols = slice((k % NS) * W, (k % NS + 1) * W)
                step = k // NS
                if k >= NS:
                    pool.wait_ge(splits, n + k - NS + 1)
                if step in (0, 3, 5):
                    src, dst = ((proj, parts[0]), None, None, (rest, parts[1]), None, (rest, parts[2]))[step]
                    pool.sem_inc(gate, 1)
                    pool.tensor_scalar(dst[:, cols], src[:, cols], 1.0, 0.0, ALU.mult, ALU.add).then_inc(splits, 1)
                elif step == 1:
                    pool.tensor_tensor(rest[:, cols], proj[:, cols], parts[0][:, cols],
                                       ALU.subtract).then_inc(splits, 1)
                elif step == 4:
                    pool.tensor_tensor(rest[:, cols], rest[:, cols], parts[1][:, cols],
                                       ALU.subtract).then_inc(splits, 1)
                else:
                    pool.tensor_tensor(proj[:, cols], proj[:, cols], proj[:, cols], ALU.mult).then_inc(splits, 1)

            def center(b, par, st):
                buf = par if st >= 0 else 1 - par
                rows = cent[buf][0:T, st % NS * SJ:(st % NS + 1) * SJ, :]
                pool.wait_ge(mean_ready, at(b, NS, st + 1))
                if st == 0:
                    pool.wait_ge(stored[par], (b - par) * 8 + 16)
                pool.tensor_tensor(rows, yb[0:T, :, :], mean[0:T, :].unsqueeze(2).broadcast_to([T, SJ, HF]),
                                   ALU.subtract).then_inc(centered, 1)
                pool.wait_ge(centered, at(b, NS, st + 1))
                pool.tensor_tensor(sq[0:T, :, :], rows, rows, ALU.mult).then_inc(squared, 1)

            def scale_rows(b, par):
                pool.wait_ge(rstd_ready, at(b, 1, 1))
                pool.tensor_tensor(cent[par][0:T, :, :], cent[par][0:T, :, :],
                                   rstd[0:T, :].unsqueeze(2).broadcast_to([T, NT, HF]), ALU.mult).then_inc(normed, 1)

            def batch(b, par, first=False, last=False):
                if not first:
                    center(b, par, -1)
                if not last:
                    pool.wait_ge(parts_out, at(b, 16 * PART_DMAS, 16 * PART_DMAS))
                    for k in range(SPLITS):
                        if k < NS:
                            pool.wait_ge(misc_free, use(b, PREP_PLACE[XT_ROUNDS + k]) + 1)
                        split(k, at(b, SPLITS, SPLITS))
                center(b, par, 0)
                if not first:
                    scale_rows(b - 1, 1 - par)
                center(b, par, 1)

            batches(pool, batch)
            center(B, 0, -1)
            scale_rows(B - 1, 1)

        @block.tensor
        def _(pe):
            def xT_round(buf, r, n):
                pe.wait_ge(misc_free, n)
                for k in range(3):
                    j = 6 * r + 2 * k
                    m = nc.tensor.transpose(misc[:, k * T:(k + 1) * T],
                                            x_sb[buf][0:T, j:j + 2, :].rearrange("p j f -> p (j f)"),
                                            ident[0:T, 0:T])
                m.then_inc(misc_full, 1)

            def proj_round(r, n):
                pe.wait_ge(misc_free, n)
                nc.tensor.matmul(misc[:, 0:W], w_proj[:, :], xT[:, r * W:(r + 1) * W],
                                 start=True, stop=True).then_inc(misc_full, 1)

            def vals_round(r, n):
                pe.wait_ge(misc_free, n)
                for c in range(8 * r, min(8 * r + 8, NT)):
                    m = nc.tensor.matmul(misc[0:T, (c - 8 * r) * HF:(c - 8 * r + 1) * HF], xT[:, c * T:(c + 1) * T],
                                         w_val[:, :], start=True, stop=True)
                m.then_inc(misc_full, 1)

            def norms_round(r, n, split_done):
                pe.wait_ge(misc_free, n)
                if r == 0:
                    pe.wait_ge(splits, split_done - 3 * NS)
                    for k in range(NS):
                        m = nc.tensor.matmul(misc[k * OW:(k + 1) * OW, 0:W], head_sum[:, :],
                                             proj[:, k * W:(k + 1) * W], start=True, stop=True,
                                             skip_group_check=True)
                else:
                    m = nc.tensor.transpose(misc[:, 0:P], norm[:, :], ident[:, :])
                m.then_inc(misc_full, 1)

            def prep_round(buf, r, n, split_done):
                if r < XT_ROUNDS:
                    xT_round(buf, r, n)
                elif r < PROJ_ROUNDS:
                    proj_round(r - XT_ROUNDS, n)
                elif r < VALS_ROUNDS:
                    vals_round(r - PROJ_ROUNDS, n)
                else:
                    norms_round(r - VALS_ROUNDS, n, split_done)

            def out_round(n):
                pe.wait_ge(misc_free, n)
                for j in range(SJ):
                    m = nc.tensor.transpose(misc[0:T, j * P:(j + 1) * P], o_sb[:, j * T:(j + 1) * T], ident[:, :])
                m.then_inc(misc_full, 1)

            pe.wait_ge(ident_ready, 1)
            pe.wait_ge(x_in, 16)
            for r in range(PREP_ROUNDS):
                if r == XT_ROUNDS:
                    pe.wait_ge(weights_in, 64)
                if r == VALS_ROUNDS:
                    pe.wait_ge(consts, CONSTS)
                prep_round(0, r, r + 1, SPLITS)

            def masks(u, par, start):
                st, c = u // UNITS, (u // H) % NT
                for j in range(SJ):
                    tile = edges[(par * NS + st) % 2][0:T + 1, j, c * T:c * T + P].bitcast(BF16)
                    m = nc.tensor.matmul(z[:, u % BANKS, j * T:(j + 1) * T],
                                         tile.rearrange("p (n two) -> p n two", two=2)[:, :, 1],
                                         edge_w[0:T + 1, :], start=start and j == 0, stop=not start,
                                         skip_group_check=True)
                return m

            def scores(u, par, start, stop):
                st, c, h = u // UNITS, (u // H) % NT, u % H
                return nc.tensor.matmul(z[:, u % BANKS, 0:W], other_st[par][0:KR, h, c * T:c * T + P],
                                        self_st[par][0:KR, h, st * W:(st + 1) * W], start=start, stop=stop,
                                        skip_group_check=True)

            def unit(u, b, par, large):
                if u % UNITS == 0:
                    pe.wait_ge(edges_in[(par * NS + u // UNITS) % 2], edges_count(b, par, u // UNITS))
                if not large and u >= BANKS and kind(u - BANKS) == "d":
                    pe.wait_ge(leaky_dve, at(b, D_UNITS, nth("d", u - BANKS)))
                else:
                    pe.wait_ge(expd, at(b, UB, u + 1))
                if kind(u) == "a" or large and kind(u) == "e":
                    scores(u, par, True, False).then_inc(scored, 1)
                else:
                    masks(u, par, True)
                    scores(u, par, False, True).then_inc(scored, 1)

            def lift(u, b, par, large):
                st, h = u // UNITS, u % H
                if kind(u) == "a":
                    pe.wait_ge(leaky_act, at(b, A_UNITS, nth("a", u)))
                elif kind(u) == "e":
                    pe.wait_ge(relu_large, at(b, E_UNITS, nth("e", u)))
                else:
                    pe.wait_ge(leaky_dve, at(b, D_UNITS, nth("d", u)))
                if kind(u) != "d":
                    scores(u, par, False, False)
                    m = masks(u, par, False)
                if large:
                    m = nc.tensor.matmul(z[:, u % BANKS, 0:W], shift_w[KR:KR + 3, :],
                                         self_st[par][KR:KR + 3, h, st * W:(st + 1) * W],
                                         start=False, stop=True, skip_group_check=True)
                m.then_inc(lifted if kind(u) == "a" else lifted_large, 1)

            def values(t, b, par):
                pe.wait_ge(expd, at(b, UB, H * (t + 1) + BANKS))
                pe.wait_ge(combined, at(b, E_UNITS, nth("e", H * t + H - 1) + LOWS))
                if t % NT == 0:
                    pe.wait_ge(numer_free, at(b, NS, t // NT + 1))
                for h in range(H):
                    m = nc.tensor.matmul(numer[h * OW:(h + 1) * OW, 0:W], vals[par][0:T, t % NT, h, :],
                                         probs[0:T, t % PROBS, h, :], start=t % NT == 0, stop=t % NT == NT - 1,
                                         skip_group_check=True)
                m.then_inc(pv_done, 1)

            def large_scores(b, par):
                pe.wait_ge(expd, at(b, UB, BANKS))
                pe.sem_inc(gate, 1)
                with pe.Fori(0, NT) as t:
                    for h in range(H):
                        pe.wait_ge(big_read, at(b, MAXIMA, h + 1) + t * H)
                        for k in range(NS):
                            m = nc.tensor.matmul(z[0:T, 3 * (h % 2) + k, 0:W],
                                                 self_st[par][0:KR, h, bass.ts(t, T)],
                                                 other_st[par][0:KR, h, k * W:(k + 1) * W], start=True, stop=True,
                                                 skip_group_check=True)
                        m.then_inc(big_scored, 1)
                pe.wait_ge(big_parts, at(b, PARTS, 3))
                nc.tensor.transpose(z[:, 0, 0:P], row_max[:, :], ident[:, :]).then_inc(big_turned, 1)
                pe.wait_ge(big_parts, at(b, PARTS, PARTS))

            def units(b, par, first, last, large):
                for u in range(UB):
                    unit(u, b, par, large)
                    if u >= LIFT_LAG and (large or kind(u - LIFT_LAG) == "a"):
                        lift(u - LIFT_LAG, b, par, large)
                    if (u - VALUES_LAG) % H == 0:
                        t = (u - VALUES_LAG) // H
                        if t >= 0:
                            values(t, b, par)
                        elif not first:
                            values(NS * NT + t, b - 1, 1 - par)
                    if u in PREP_AT and not last:
                        n = PREP_AT.index(u)
                        if n == 0:
                            pe.wait_ge(x_in, at(b, 16, 32))
                        prep_round(1 - par, n, use(b, PREP_PLACE[n]), at(b, SPLITS, 2 * SPLITS))
                    if u % UNITS == OUT_AT and not (first and u == OUT_AT):
                        k = u // UNITS
                        pe.wait_ge(numer_free, at(b, NS, k + 1))
                        out_round(use(b, (OUT_PLACE_LAST if last else OUT_PLACE)[k]))
                for u in range(UB - LIFT_LAG, UB):
                    if large or kind(u) == "a":
                        lift(u, b, par, large)

            def batch(b, par, first=False, last=False):
                pe.wait_ge(stacks_in, at(b, 16 * STACK_DMAS, 16 * STACK_DMAS))
                pe.wait_ge(safe_ready, at(b, 1, 1))
                pe.sem_inc(gate, 1)
                small = pe.value_load(safe[par][0:1, 0:1], min_val=0, max_val=1)
                with pe.If(small == 0):
                    large_scores(b, par)
                    pe.wait_ge(shift_in, at(b, 16 * 3, 16 * 3))
                    units(b, par, first, last, large=True)
                with pe.Else():
                    pe.sem_inc(big_scored, MAXIMA)
                    pe.sem_inc(big_turned, 1)
                    pe.sem_inc(relu_large, E_UNITS)
                    units(b, par, first, last, large=False)

            batches(pe, batch)
            for t in range(-(VALUES_LAG // H), 0):
                values(NS * NT + t, B - 1, 1)
            pe.wait_ge(numer_free, at(B, NS, 1))
            out_round(use(B - 1, NS + 1))

        @block.scalar
        def _(act):
            act.sem_inc(expd, BANKS)

            def relu(u, b):
                bank = z[0:T, u % BANKS, 0:W]
                act.wait_ge(scored, at(b, UB, u + 1))
                nc.scalar.activation(bank, bank, ACT.Relu, scale=GAIN
                                     ).then_inc(leaky_act if kind(u) == "a" else relu_large, 1)

            def units(b, large):
                for v in range(UB + RELU_LEAD):
                    if v < UB and (kind(v) == "a" or large and kind(v) == "e"):
                        relu(v, b)
                    u = v - RELU_LEAD
                    if u < 0:
                        continue
                    if kind(u) == "a":
                        act.wait_ge(lifted, at(b, A_UNITS, nth("a", u)))
                    elif large:
                        act.wait_ge(lifted_large, at(b, D_UNITS + E_UNITS, nth("de", u)))
                    elif kind(u) == "d":
                        act.wait_ge(leaky_dve, at(b, D_UNITS, nth("d", u)))
                    else:
                        act.wait_ge(scored, at(b, UB, u + 1))
                    if u % H == 0:
                        act.wait_ge(pv_done, at(b, NS * NT, u // H + 1))
                    bank, prob = z[0:T, u % BANKS, 0:W], probs[0:T, (u // H) % PROBS, u % H, :]
                    if kind(u) == "e":
                        nc.scalar.activation(prob, bank, ACT.Exp, scale=LOW if large else HIGH)
                        e = nth("e", u)
                        act.wait_ge(combined, at(b, E_UNITS, e))
                        nc.scalar.activation(low[0:T, (e - 1) % LOWS, :], bank, ACT.Exp, scale=LOW).then_inc(expd, 1)
                    else:
                        if kind(u) == "d" and not large:
                            bank = leak[0:T, nth("d", u) % LEAKS, :]
                        nc.scalar.activation(prob, bank, ACT.Exp, scale=LOW).then_inc(expd, 1)

            def batch(b, par, first=False, last=False):
                act.wait_ge(safe_ready, at(b, 1, 1))
                act.sem_inc(gate, 1)
                small = act.value_load(safe[par][0:1, 0:1], min_val=0, max_val=1)
                with act.If(small == 0):
                    units(b, large=True)
                with act.Else():
                    act.sem_inc(lifted_large, D_UNITS + E_UNITS)
                    units(b, large=False)

            batches(act, batch)

        @block.vector
        def _(dve):
            dve.sem_inc(resid, 1)
            dve.sem_inc(big_read, 2)
            dve.sem_inc(misc_free, 1)
            dve.sem_inc(numer_free, 1)
            dve.sem_inc(pv_done, PROBS)
            dve.sem_inc(combined, LOWS)

            def split(k):
                cols = slice((k % NS) * W, (k % NS + 1) * W)
                step = k // NS
                if k >= NS:
                    dve.wait_ge(splits, k - NS + 1)
                if step in (0, 3, 5):
                    src, dst = ((proj, parts[0]), None, None, (rest, parts[1]), None, (rest, parts[2]))[step]
                    if step == 0:
                        dve.wait_ge(misc_free, XT_ROUNDS + k + 2)
                    nc.vector.tensor_copy(dst[:, cols], src[:, cols]).then_inc(splits, 1)
                elif step == 1:
                    nc.vector.tensor_tensor(rest[:, cols], proj[:, cols], parts[0][:, cols],
                                            ALU.subtract).then_inc(splits, 1)
                elif step == 4:
                    nc.vector.tensor_tensor(rest[:, cols], rest[:, cols], parts[1][:, cols],
                                            ALU.subtract).then_inc(splits, 1)
                else:
                    nc.vector.tensor_tensor(proj[:, cols], proj[:, cols], proj[:, cols], ALU.mult).then_inc(splits, 1)

            def take(buf, r, n, flags):
                dve.wait_ge(misc_full, n)
                if r < XT_ROUNDS:
                    for k in range(2):
                        m = nc.vector.tensor_copy(
                            xT[:, 6 * T * r:6 * T * (r + 1)].rearrange("f (j k n) -> f j k n", k=2, n=T)[:, :, k, :],
                            misc[k * F:(k + 1) * F, 0:3 * T].rearrange("f (j n) -> f j n", n=T))
                    m.then_inc(misc_free, 1)
                elif r < PROJ_ROUNDS:
                    s0 = (r - XT_ROUNDS) * W
                    nc.vector.tensor_copy(proj[:, s0:s0 + W], misc[:, 0:W]).then_inc(misc_free, 1)
                elif r < VALS_ROUNDS:
                    c0 = 8 * (r - PROJ_ROUNDS)
                    c1 = min(c0 + 8, NT)
                    nc.vector.tensor_copy(vals[buf][0:T, c0:c1, :, 0:D],
                                          misc[0:T, 0:(c1 - c0) * HF].rearrange("p (c h d) -> p c h d", c=c1 - c0, h=H)
                                          ).then_inc(misc_free, 1)
                elif r == VALS_ROUNDS:
                    nc.vector.reduce_max(norm[0:NS * OW, 0:1], misc[0:NS * OW, 0:W], axis=AX_X).then_inc(misc_free, 1)
                else:
                    nc.vector.reduce_max(flag_f[0:1, 0:2 * H],
                                         misc[0:1, 0:NS * OW].rearrange("p (k c) -> p c k", c=OW)[:, 0:2 * H, :],
                                         axis=AX_X).then_inc(misc_free, 1)
                    dve.wait_ge(misc_free, n + 1)
                    nc.vector.reduce_max(flag_f[0:1, 2 * H:2 * H + 2],
                                         flag_f[0:1, 0:2 * H].rearrange("p (k h) -> p k h", h=H),
                                         axis=AX_X).then_inc(flag, 1)
                    dve.wait_ge(flag, flags + 1)
                    nc.vector.tensor_tensor(flag_f[0:1, 2 * H + 2:2 * H + 3], flag_f[0:1, 2 * H:2 * H + 1],
                                            flag_f[0:1, 2 * H + 1:2 * H + 2], ALU.mult).then_inc(flag, 1)
                    dve.wait_ge(flag, flags + 2)
                    nc.vector.tensor_scalar(flag_f[0:1, 2 * H + 3:2 * H + 4], flag_f[0:1, 2 * H + 2:2 * H + 3],
                                            1.0 / 16, SAFE * SAFE, ALU.mult, ALU.is_le).then_inc(flag, 1)
                    dve.wait_ge(flag, flags + 3)
                    nc.vector.tensor_copy(safe[buf][0:1, 0:1], flag_f[0:1, 2 * H + 3:2 * H + 4]).then_inc(safe_ready, 1)

            def large_scores(b):
                with dve.Fori(0, NT) as t:
                    dve.wait_ge(big_adj_in, at(b, 16 * NT, 16) + t * 16)
                    nc.vector.tensor_scalar(rest[0:T, :], rest[0:T, :], -1.0, BIG,
                                            ALU.add, ALU.mult).then_inc(big_max, 1)
                    for h in range(H):
                        dve.wait_ge(big_max, at(b, MAXIMA + NT, h + 1) + t * (H + 1))
                        dve.wait_ge(big_scored, at(b, MAXIMA, h + 1) + t * H)
                        nc.vector.tensor_tensor(proj[0:T, :].rearrange("p (k n) -> p k n", k=NS),
                                                z[0:T, 3 * (h % 2):3 * (h % 2) + 3, 0:W],
                                                rest[0:T, :].rearrange("p (k n) -> p k n", k=NS),
                                                ALU.add).then_inc(big_read, 1)
                        dve.wait_ge(big_read, at(b, MAXIMA, h + 3) + t * H)
                        nc.vector.reduce_max(row_max[0:T, bass.ds(h * NT + t, 1)], proj[0:T, :],
                                             axis=AX_X).then_inc(big_max, 1)
                mx, tmp = row_max[0:T, 0:MAXIMA], row_tmp[0:T, 0:MAXIMA]
                dve.wait_ge(big_max, at(b, MAXIMA + NT, MAXIMA + NT))
                nc.vector.tensor_scalar(tmp, mx, -BIG / 1024, None, ALU.is_gt).then_inc(big_parts, 1)
                dve.wait_ge(big_parts, at(b, PARTS, 1))
                nc.vector.scalar_tensor_tensor(tmp, mx, -1.0, tmp, ALU.mult, ALU.mult).then_inc(big_parts, 1)
                dve.wait_ge(big_parts, at(b, PARTS, 2))
                nc.vector.scalar_tensor_tensor(mx, tmp, 1.0 + GAIN, tmp, ALU.mult, ALU.min).then_inc(big_parts, 1)
                dve.wait_ge(big_turned, at(b, 1, 1))
                turned, left = z[0:MAXIMA, 0, 0:T], row_tmp[0:MAXIMA, 0:T]
                nc.vector.tensor_copy(max_part[0][:, :], turned).then_inc(big_parts, 1)
                dve.wait_ge(big_parts, at(b, PARTS, 4))
                nc.vector.tensor_tensor(left, turned, max_part[0][:, :], ALU.subtract).then_inc(big_parts, 1)
                dve.wait_ge(big_parts, at(b, PARTS, 5))
                nc.vector.tensor_copy(max_part[1][:, :], left).then_inc(big_parts, 1)
                dve.wait_ge(big_parts, at(b, PARTS, 6))
                nc.vector.tensor_tensor(max_part[2][:, :], left, max_part[1][:, :],
                                        ALU.subtract).then_inc(big_parts, 1)

            def relu(u, b, first):
                bank, n = z[0:T, u % BANKS, 0:W], nth("d", u)
                dve.wait_ge(scored, at(b, UB, u + 1))
                if n > LEAKS:
                    dve.wait_ge(expd, at(b, UB, BANKS + 1 + D_PLACES[n - LEAKS - 1]))
                elif not first:
                    dve.wait_ge(expd, at(b, UB, BANKS + 1 - UB + D_PLACES[n - LEAKS - 1]))
                nc.vector.tensor_scalar(leak[0:T, n % LEAKS, :], bank, 0.0, GAIN,
                                        ALU.max, ALU.mult).then_inc(half, 1)

            def add(u, b, large):
                bank, n = z[0:T, u % BANKS, 0:W], nth("d", u)
                dve.wait_ge(half, at(b, D_UNITS, n))
                nc.vector.tensor_tensor(bank if large else leak[0:T, n % LEAKS, :], bank, leak[0:T, n % LEAKS, :],
                                        ALU.add).then_inc(leaky_dve, 1)

            def combine(u, b):
                n = nth("e", u)
                prob = probs[0:T, (u // H) % PROBS, u % H, :]
                dve.wait_ge(expd, at(b, UB, BANKS + u + 1))
                nc.vector.tensor_tensor(prob, prob, low[0:T, (n - 1) % LOWS, :], ALU.max).then_inc(combined, 1)

            def finish(step, st, b, par, misc_n):
                buf, t0 = par if st >= 0 else 1 - par, st % NS * SJ
                summed = misc[0:T, 0:SJ * P].rearrange("p (j c) -> p j c", c=OW)
                if step == 0:
                    dve.wait_ge(pv_done, at(b, NS * NT, (st + 1) * NT + PROBS))
                    nc.vector.tensor_copy(o_sb[:, :], numer[:, 0:W]).then_inc(numer_free, 1)
                elif step == 1:
                    dve.wait_ge(misc_full, misc_n)
                    nc.vector.tensor_scalar(den[0:T, :], summed[:, :, D], 1e-30, None, ALU.max).then_inc(epi, 1)
                elif step == 2:
                    dve.wait_ge(epi, at(b, 4 * NS, 4 * st + 1))
                    nc.vector.reciprocal(rden[0:T, :], den[0:T, :]).then_inc(epi, 1)
                elif step == 3:
                    dve.wait_ge(epi, at(b, 4 * NS, 4 * st + 2))
                    nc.vector.tensor_tensor(ob[0:T, :, :].rearrange("p j (h d) -> p (j h) d", d=D),
                                            summed[:, :, 0:D],
                                            rden[0:T, :].unsqueeze(2).broadcast_to([T, SJ * H, D]),
                                            ALU.mult).then_inc(misc_free, 1)
                elif step == 4:
                    dve.wait_ge(misc_free, misc_n + 1)
                    nc.vector.tensor_tensor(ob[0:T, :, :], ob[0:T, :, :],
                                            bias_rep[0:T, :].unsqueeze(1).broadcast_to([T, SJ, HF]),
                                            ALU.add).then_inc(epi, 1)
                elif step == 5:
                    dve.wait_ge(epi, at(b, 4 * NS, 4 * st + 3))
                    nc.vector.scalar_tensor_tensor(yb[0:T, :, :], ob[0:T, :, :], 0.0,
                                                   x_sb[buf][0:T, t0:t0 + SJ, :], ALU.max,
                                                   ALU.add).then_inc(resid, 1)
                elif step == 6:
                    dve.wait_ge(resid, at(b, NS, st + 2))
                    nc.vector.reduce_sum(mean[0:T, :], yb[0:T, :, :], axis=AX_X).then_inc(epi, 1)
                elif step == 7:
                    dve.wait_ge(epi, at(b, 4 * NS, 4 * st + 4))
                    nc.vector.tensor_scalar(mean[0:T, :], mean[0:T, :], 1.0 / HF, None,
                                            ALU.mult).then_inc(mean_ready, 1)
                elif step == 8:
                    dve.wait_ge(squared, at(b, NS, st + 1))
                    nc.vector.reduce_sum(var[0:T, t0:t0 + SJ], sq[0:T, :, :],
                                         axis=AX_X).then_inc(newton, 1)

            def inverse_root(step, b):
                v, y, t = var[0:T, :], rstd[0:T, :], nwt[0:T, :]
                dve.wait_ge(newton, at(b, NEWTON, NS + step))
                if step == 0:
                    nc.vector.tensor_scalar(v, v, 1.0 / HF, EPS, ALU.mult, ALU.add).then_inc(newton, 1)
                elif step == 1:
                    nc.vector.tensor_scalar(t.bitcast(I32), v.bitcast(I32), 1, None,
                                            ALU.logical_shift_right).then_inc(newton, 1)
                elif step == 2:
                    dve.wait_ge(normed, at(b, 1, 1))
                    nc.vector.tensor_scalar(y.bitcast(I32), t.bitcast(I32), -1.0, float(0x5F3759DF),
                                            ALU.mult, ALU.add).then_inc(newton, 1)
                elif step % 3 == 0:
                    nc.vector.tensor_tensor(t, y, y, ALU.mult).then_inc(newton, 1)
                elif step % 3 == 1:
                    nc.vector.scalar_tensor_tensor(t, t, -0.5, v, ALU.mult, ALU.mult).then_inc(newton, 1)
                else:
                    nc.vector.scalar_tensor_tensor(y, t, 1.5, y, ALU.add, ALU.mult
                                                   ).then_inc(rstd_ready if step == ROOT - 1 else newton, 1)

            for r in range(PREP_ROUNDS):
                if r == PROJ_ROUNDS:
                    for k in range(3 * NS):
                        split(k)
                    dve.wait_ge(vals_init, 4)
                if r == VALS_ROUNDS:
                    for k in range(5 * NS, SPLITS):
                        split(k)
                    dve.wait_ge(pads, 3)
                if r == PROJ_ROUNDS + 1:
                    for k in range(3 * NS, 5 * NS):
                        split(k)
                take(0, r, r + 1, 0)

            def batch(b, par, first=False, last=False):
                dve.wait_ge(safe_ready, at(b, 1, 1))
                dve.sem_inc(gate, 1)
                small = dve.value_load(safe[par][0:1, 0:1], min_val=0, max_val=1)
                with dve.If(small == 0):
                    large_scores(b)
                    units(b, par, first, last, large=True)
                with dve.Else():
                    dve.sem_inc(big_read, MAXIMA)
                    dve.sem_inc(big_max, MAXIMA + NT)
                    dve.sem_inc(big_parts, PARTS)
                    units(b, par, first, last, large=False)

            def units(b, par, first, last, large):
                for u in range(UB):
                    if kind(u) == "d":
                        relu(u, b, first)
                        add(u, b, large)
                    if kind(u - COMBINE_LAG) == "e":
                        if u >= COMBINE_LAG:
                            combine(u - COMBINE_LAG, b)
                        elif not first:
                            combine(UB + u - COMBINE_LAG, b - 1)
                    if u - TAKE_LAG in PREP_AT and not last:
                        n = PREP_AT.index(u - TAKE_LAG)
                        take(1 - par, n, use(b, PREP_PLACE[n]), at(b, 3, 3))
                    k = u // UNITS
                    if u % UNITS in FINISH_AT and not (first and k == 0):
                        finish(FINISH_AT.index(u % UNITS), k - 1, b, par,
                               use(b, (OUT_PLACE_LAST if last else OUT_PLACE)[k]))
                    if u - ROOT_AT in range(0, 2 * ROOT, 2) and not first:
                        inverse_root((u - ROOT_AT) // 2, b - 1)

            batches(dve, batch)
            for u in range(UB - COMBINE_LAG, UB):
                if kind(u) == "e":
                    combine(u, B - 1)
            for step in range(len(FINISH_AT)):
                finish(step, -1, B, 0, use(B - 1, NS + 1))
            for step in range(ROOT):
                inverse_root(step, B - 1)


_INS = ["x", "adj", "L0_gnn_kernel", "L0_gnn_attention_kernel", "L0_gnn_attention_kernel_2", "L0_gnn_bias"]


def kernel(**inputs):
    import numpy as _np
    import concourse.bacc as _bacc
    from concourse import mybir as _mybir
    from concourse.bass_utils import run_bass_kernel_spmd as _run

    nc = _bacc.Bacc("TRN2", target_bir_lowering=False, num_devices=1)
    arrays, args = {}, []
    for name in _INS:
        a = _np.ascontiguousarray(inputs[name])
        arrays[f"in_{name}"] = a
        args.append(nc.dram_tensor(f"in_{name}", a.shape, _mybir.dt.from_np(a.dtype), kind="ExternalInput").ap())
    out = nc.dram_tensor("out", (B, N, F), F32, kind="ExternalOutput").ap()
    gat_layer(nc, *args, out)
    r = _run(nc, [arrays], core_ids=[0])
    return r.results[0]["out"]
```
